# Optimizing a Trainium2 kernel written in Bass

```python
import numpy as np
import jax
import jax.numpy as jnp

def _softmax(x, axis=-1):
    return jax.nn.softmax(x, axis=axis)

def _gelu(x):
    return jax.nn.gelu(x, approximate=True)

def _silu(x):
    return jax.nn.silu(x)

def _sigmoid(x):
    return jax.nn.sigmoid(x)

def _layernorm(x, axis=-1, eps=1e-05):
    m = jnp.mean(x, axis=axis, keepdims=True)
    v = jnp.var(x, axis=axis, keepdims=True)
    return (x - m) / jnp.sqrt(v + eps)

def _scatter_add(tgt, idx, src, axis=0):
    return tgt.at[idx].add(src)

def _segment_sum(src, seg, n):
    return jax.ops.segment_sum(src, seg, n)
kernel_name = 'mk_gnn_preln_d2_gnn_r8_997d68'

def setup_inputs(seed: int=0):
    np.random.seed(seed)
    _w = jnp.asarray

    def _rec_inputs():
        import jax
        import jax.numpy as jnp
        _gk = jax.random.key(seed)
        x = -0.000202 + 1 * jax.random.normal(jax.random.fold_in(_gk, 1), (6250, 128), jnp.float32)
        src = jax.random.randint(jax.random.fold_in(_gk, 2), (100000,), 0, 6250, jnp.int32)
        dst = jnp.minimum((6250 * jax.random.uniform(jax.random.fold_in(_gk, 3), (100000,)) ** 2.0).astype(jnp.int32), 49999)
        _o = jnp.argsort(dst, stable=True)
        src = src[_o]
        dst = dst[_o]
        edge_attr_128 = 7.68618e-05 + 1.00005 * jax.random.normal(jax.random.fold_in(_gk, 11), (100000, 128), jnp.float32)
        return (x, src, dst, edge_attr_128)
    x, src, dst, edge_attr_128 = _rec_inputs()

    def _L0_gnn_setup():
        import jax, jax.numpy as jnp
        import numpy as np
        N_NODES = 6250
        BN_EPS = 1e-05

        def _gine_layer(x, src, dst, edge_attr, W1l, b1l, gl, bl, W2l, b2l):
            msg = jax.nn.relu(x[src] + edge_attr)
            agg = jax.ops.segment_sum(msg, dst, num_segments=N_NODES)
            h = (x + agg) @ W1l + b1l
            mu = jnp.mean(h, axis=0)
            var = jnp.mean(jnp.square(h - mu), axis=0)
            h = (h - mu) * jax.lax.rsqrt(var + BN_EPS) * gl + bl
            h = jax.nn.relu(h)
            h = jax.nn.relu(h @ W2l + b2l)
            return jax.nn.relu(h)
        key = jax.random.key(seed)
        ks = jax.random.split(key, 10)
        n, e, d, L = (N_NODES, 62500, 128, 2)
        x = jax.random.normal(ks[0], (n, d), dtype=jnp.float32)
        edge_index = jax.random.randint(ks[1], (2, e), 0, n, dtype=jnp.int64)
        edge_attr = jax.random.normal(ks[2], (e, d), dtype=jnp.float32)
        W1 = jax.random.normal(ks[3], (L, d, d), dtype=jnp.float32) * 0.05
        b1 = jax.random.normal(ks[4], (L, d), dtype=jnp.float32) * 0.02
        gamma = 1.0 + 0.1 * jax.random.normal(ks[5], (L, d), dtype=jnp.float32)
        beta = 0.1 * jax.random.normal(ks[6], (L, d), dtype=jnp.float32)
        W2 = jax.random.normal(ks[7], (L, d, d), dtype=jnp.float32) * 0.05
        b2 = jax.random.normal(ks[8], (L, d), dtype=jnp.float32) * 0.02
        return {'x': x, 'edge_index': edge_index, 'edge_attr': edge_attr, 'W1': W1, 'b1': b1, 'gamma': gamma, 'beta': beta, 'W2': W2, 'b2': b2}
    _L0_gnn_all = _L0_gnn_setup()
    _L0_gnn_in = {k: v for k, v in _L0_gnn_all.items() if k in ('W1', 'b1', 'gamma', 'beta', 'W2', 'b2')}
    del _L0_gnn_all

    def _L1_gnn_setup():
        import jax, jax.numpy as jnp
        import numpy as np
        N_NODES = 6250
        N_EDGES = 100000
        D = 128

        def _gin_conv(x, edge_index, wA, bA, wB, bB, eps):
            src, dst = (edge_index[0], edge_index[1])
            agg = jax.ops.segment_sum(x[src], dst, num_segments=x.shape[0])
            h = (1.0 + eps) * x + agg
            h = jax.nn.relu(h @ wA.T + bA) @ wB.T + bB
            return h
        key = jax.random.key(seed)
        ks = jax.random.split(key, 8)
        std = 1.0 / np.sqrt(D)
        inp = {'features': jax.random.normal(ks[0], (N_NODES, D), dtype=jnp.float32), 'edge_index': jax.random.randint(ks[1], (2, N_EDGES), 0, N_NODES, dtype=jnp.int64), 'w1a': jax.random.normal(ks[2], (D, D), dtype=jnp.float32) * std, 'b1a': jnp.zeros((D,), dtype=jnp.float32), 'w1b': jax.random.normal(ks[3], (D, D), dtype=jnp.float32) * std, 'b1b': jnp.zeros((D,), dtype=jnp.float32), 'eps1': jnp.float32(0.0), 'w2a': jax.random.normal(ks[4], (D, D), dtype=jnp.float32) * std, 'b2a': jnp.zeros((D,), dtype=jnp.float32), 'w2b': jax.random.normal(ks[5], (D, D), dtype=jnp.float32) * std, 'b2b': jnp.zeros((D,), dtype=jnp.float32), 'eps2': jnp.float32(0.0)}
        return inp
    _L1_gnn_all = _L1_gnn_setup()
    _L1_gnn_in = {k: v for k, v in _L1_gnn_all.items() if k in ('w1a', 'b1a', 'w1b', 'b1b', 'eps1', 'w2a', 'b2a', 'w2b', 'b2b', 'eps2')}
    del _L1_gnn_all
    return {'x': x, 'src': src, 'dst': dst, 'edge_attr_128': edge_attr_128, 'L0_gnn_W1': _L0_gnn_in['W1'], 'L0_gnn_b1': _L0_gnn_in['b1'], 'L0_gnn_gamma': _L0_gnn_in['gamma'], 'L0_gnn_beta': _L0_gnn_in['beta'], 'L0_gnn_W2': _L0_gnn_in['W2'], 'L0_gnn_b2': _L0_gnn_in['b2'], 'L1_gnn_w1a': _L1_gnn_in['w1a'], 'L1_gnn_b1a': _L1_gnn_in['b1a'], 'L1_gnn_w1b': _L1_gnn_in['w1b'], 'L1_gnn_b1b': _L1_gnn_in['b1b'], 'L1_gnn_eps1': _L1_gnn_in['eps1'], 'L1_gnn_w2a': _L1_gnn_in['w2a'], 'L1_gnn_b2a': _L1_gnn_in['b2a'], 'L1_gnn_w2b': _L1_gnn_in['w2b'], 'L1_gnn_b2b': _L1_gnn_in['b2b'], 'L1_gnn_eps2': _L1_gnn_in['eps2']}

def reference(x, src, dst, edge_attr_128, L0_gnn_W1, L0_gnn_b1, L0_gnn_gamma, L0_gnn_beta, L0_gnn_W2, L0_gnn_b2, L1_gnn_w1a, L1_gnn_b1a, L1_gnn_w1b, L1_gnn_b1b, L1_gnn_eps1, L1_gnn_w2a, L1_gnn_b2a, L1_gnn_w2b, L1_gnn_b2b, L1_gnn_eps2):
    import jax
    import jax.numpy as jnp

    def _L0_gnn_ref(x, edge_index, edge_attr, W1, b1, gamma, beta, W2, b2):
        import jax, jax.numpy as jnp
        import numpy as np
        N_NODES = 6250
        BN_EPS = 1e-05

        def _gine_layer(x, src, dst, edge_attr, W1l, b1l, gl, bl, W2l, b2l):
            msg = jax.nn.relu(x[src] + edge_attr)
            agg = jax.ops.segment_sum(msg, dst, num_segments=N_NODES)
            h = (x + agg) @ W1l + b1l
            mu = jnp.mean(h, axis=0)
            var = jnp.mean(jnp.square(h - mu), axis=0)
            h = (h - mu) * jax.lax.rsqrt(var + BN_EPS) * gl + bl
            h = jax.nn.relu(h)
            h = jax.nn.relu(h @ W2l + b2l)
            return jax.nn.relu(h)
        src, dst = (edge_index[0], edge_index[1])
        L = W1.shape[0]
        for l in range(L):
            x = _gine_layer(x, src, dst, edge_attr, W1[l], b1[l], gamma[l], beta[l], W2[l], b2[l])
        return x

    def _L1_gnn_ref(features, edge_index, w1a, b1a, w1b, b1b, eps1, w2a, b2a, w2b, b2b, eps2):
        import jax, jax.numpy as jnp
        import numpy as np
        N_NODES = 6250
        N_EDGES = 100000
        D = 128

        def _gin_conv(x, edge_index, wA, bA, wB, bB, eps):
            src, dst = (edge_index[0], edge_index[1])
            agg = jax.ops.segment_sum(x[src], dst, num_segments=x.shape[0])
            h = (1.0 + eps) * x + agg
            h = jax.nn.relu(h @ wA.T + bA) @ wB.T + bB
            return h
        x = jax.nn.relu(_gin_conv(features, edge_index, w1a, b1a, w1b, b1b, eps1))
        x = _gin_conv(x, edge_index, w2a, b2a, w2b, b2b, eps2)
        return x
    edge_index = jnp.stack([src, dst])
    h = jnp.maximum(_layernorm(x, axis=-1), 0.0)
    x = x + _L0_gnn_ref(h, edge_index, edge_attr_128, L0_gnn_W1, L0_gnn_b1, L0_gnn_gamma, L0_gnn_beta, L0_gnn_W2, L0_gnn_b2)
    h = jnp.maximum(_layernorm(x, axis=-1), 0.0)
    x = x + _L1_gnn_ref(h, edge_index, L1_gnn_w1a, L1_gnn_b1a, L1_gnn_w1b, L1_gnn_b1b, L1_gnn_eps1, L1_gnn_w2a, L1_gnn_b2a, L1_gnn_w2b, L1_gnn_b2b, L1_gnn_eps2)
    return x

_drawn_inputs = setup_inputs


def setup_inputs(seed=0):
    import zlib

    import numpy as np

    out = dict(_drawn_inputs(seed))
    spreads = {'L1_gnn_b1a': (0.0, 0.8),
     'L1_gnn_b1b': (0.0, 0.447),
     'L1_gnn_b2a': (0.0, 0.8),
     'L1_gnn_b2b': (0.0, 0.8)}
    factors = {'edge_attr_128': 8.0,
     'L0_gnn_b1': 8.0,
     'L0_gnn_gamma': 6.108,
     'L0_gnn_beta': 2.954,
     'L0_gnn_b2': 3.635}
    for name, (base, spread) in spreads.items():
        noise = np.random.default_rng([zlib.crc32(name.encode()), seed]).standard_normal(out[name].shape)
        drawn = base * np.exp(spread * noise) if base else spread * noise
        out[name] = jnp.asarray(drawn.astype(out[name].dtype))
    for name, factor in factors.items():
        out[name] = (out[name] * factor).astype(out[name].dtype)
    return out
```

```python
from contextlib import ExitStack

import concourse.bass as bass
from concourse import mybir

ALU = mybir.AluOpType
ACT = mybir.ActivationFunctionType
AX_X = mybir.AxisListType.X
F32 = mybir.dt.float32
I32 = mybir.dt.int32

P = 128
NODES = 6250
EDGES = 100000
D = 128
EPP = 4
SUP = P * EPP
SUPERS = -(-EDGES // SUP)
TAIL_START = EDGES - SUP
OVERLAP = SUPERS * SUP - EDGES
SLOTS = 4
TURNS = SUPERS // SLOTS
WIN = 128
BLOCKS = -(-NODES // P)
PADDED = BLOCKS * P
ACC = PADDED + WIN
GB = 4
GROUPS = -(-BLOCKS // GB)
FIRST = P
SECOND = SUPERS - FIRST
LAST_BLOCK = NODES - (BLOCKS - 1) * P
LN_EPS = 1e-5
BN_EPS = 1e-5
LAYERS = 4

assert SUPERS % SLOTS == 0 and OVERLAP % EPP == 0 and SECOND <= P


def group_blocks(g):
    return range(g * GB, min((g + 1) * GB, BLOCKS))


def group_cols(g):
    return g * GB * P, len(group_blocks(g)) * P


def real_cols(g):
    c0, n = group_cols(g)
    return min(n, NODES - c0)


def gnn_kernel(nc, x, src, dst, edge_attr, W1, b1, gamma, beta, W2, b2,
               w1a, b1a, w1b, b1b, eps1, w2a, b2a, w2b, b2b, eps2, out):
    with ExitStack() as ctx:
        ctx.enter_context(nc.allow_non_contiguous_dma(reason="columns of biases"))

        def sb(name, shape, dt=F32):
            return ctx.enter_context(nc.sbuf_tensor(name, shape, dt))

        def sem(name):
            return ctx.enter_context(nc.semaphore(name))

        table = nc.dram_tensor("node_table", [PADDED, D], F32, kind="Internal").ap()

        ident = sb("ident", [P, P])
        iota0 = sb("iota0", [P, WIN])
        w_first = sb("w_first", [P, LAYERS, D])
        w_second = sb("w_second", [P, LAYERS, D])
        w_rows = sb("w_rows", [P, 4, D])
        bias_first = sb("bias_first", [P, LAYERS])
        bias_second = sb("bias_second", [P, LAYERS])
        bn_gamma = sb("bn_gamma", [P, 2])
        bn_beta = sb("bn_beta", [P, 2])
        eps_col = sb("eps_col", [P, 2])
        one_eps = sb("one_eps", [P, 2])
        small_eps = sb("small_eps", [P, 1])
        raw = sb("raw", [P, 4, SUP], I32)
        flt = sb("flt", [P, 4, SUP])
        win_stat = sb("win_stat", [P, 2, 3])
        src_all = sb("src_all", [P, SUPERS + SLOTS, EPP], I32)
        loc_all = sb("loc_all", [P, SUPERS, EPP])
        base_f = sb("base_f", [1, SUPERS])
        spread_f = sb("spread_f", [1, 2])
        cur_base_f = sb("cur_base_f", [1, SUPERS])
        cur_base = sb("cur_base", [1, SUPERS], I32)
        cur_iota = sb("cur_iota", [P, WIN])
        rounds_i = sb("rounds_i", [1, 2], I32)
        rows_x = sb("rows_x", [P, BLOCKS, D])
        rows_h = sb("rows_h", [P, BLOCKS, D])
        acc = sb("acc", [P, ACC])
        hid = sb("hid", [P, PADDED])
        ln_stats = sb("ln_stats", [P, BLOCKS, 6])
        ln_mv = sb("ln_mv", [P, BLOCKS, 2])
        ln_rstd = sb("ln_rstd", [P, BLOCKS])
        bn_stats = sb("bn_stats", [P, GROUPS, 6])
        bn_mv = sb("bn_mv", [P, 2])
        bn_std = sb("bn_std", [P, 1])
        bn_scale = sb("bn_scale", [P, 1])
        bn_shift = sb("bn_shift", [P, 1])
        bn_tmp = sb("bn_tmp", [P, 1])
        idx = sb("idx", [P, SLOTS, EPP], I32)
        xg = sb("xg", [P, SLOTS, EPP, D])
        ea = sb("ea", [P, SLOTS, EPP, D])
        hot = sb("hot", [P, SLOTS, EPP, WIN])

        psW = ctx.enter_context(nc.psum_tensor("psW", [P, SLOTS, 512], F32))
        psG = ctx.enter_context(nc.psum_tensor("psG", [P, 4, 512], F32))

        params_loaded = sem("params_loaded")
        x_loaded = [sem(f"x_loaded{g}") for g in range(GROUPS)]
        src_loaded = sem("src_loaded")
        dst_loaded = sem("dst_loaded")
        consts_made = sem("consts_made")
        pad_cleared = sem("pad_cleared")
        weights_turned = sem("weights_turned")
        weights_ready = sem("weights_ready")
        src_float = sem("src_float")
        src_turned = sem("src_turned")
        src_ready = sem("src_ready")
        loc_float = sem("loc_float")
        loc_turned = sem("loc_turned")
        loc_ready = sem("loc_ready")
        stat_ready = sem("stat_ready")
        base_turned = sem("base_turned")
        rounds_ready = sem("rounds_ready")
        vec = sem("vec")
        ln_var_ready = sem("ln_var_ready")
        ln_std_ready = sem("ln_std_ready")
        normed = sem("normed")
        rows_ready = sem("rows_ready")
        table_written = sem("table_written")
        cols_turned = sem("cols_turned")
        cols_ready = sem("cols_ready")
        first_done = sem("first_done")
        hid_ready = sem("hid_ready")
        bn_var_ready = sem("bn_var_ready")
        bn_std_ready = sem("bn_std_ready")
        bn_ready = sem("bn_ready")
        act_ready = sem("act_ready")
        second_done = sem("second_done")
        next_ready = sem("next_ready")
        rows_turned = sem("rows_turned")
        acc_scaled = sem("acc_scaled")
        resid_ready = sem("resid_ready")
        round_step = sem("round_step")
        slots_opened = sem("slots_opened")
        rounds_opened = sem("rounds_opened")
        bn_step = sem("bn_step")
        out_written = sem("out_written")

        idx_ready = [sem(f"idx_ready{u}") for u in range(SLOTS)]
        gathered = [[sem(f"gathered{u}_{j}") for j in range(EPP)] for u in range(SLOTS)]
        ea_loaded = [sem(f"ea_loaded{u}") for u in range(SLOTS)]
        summed = [sem(f"summed{u}") for u in range(SLOTS)]
        reduced = [sem(f"reduced{u}") for u in range(SLOTS)]
        added = [sem(f"added{u}") for u in range(SLOTS)]
        msg_ready = [sem(f"msg_ready{u}") for u in range(SLOTS)]
        hot_ready = [sem(f"hot_ready{u}") for u in range(SLOTS)]

        table_b = table.rearrange("(b p) d -> p b d", p=P)
        LG = GROUPS
        PARAMS = 16 * (2 * 6 + 4 + 4 + 2)

        def turns_before(eng, rounds, layer, r):
            return eng.snap((rounds * layer + r) * TURNS)

        block = ctx.enter_context(nc.Block())

        @block.sync
        def _(sp):
            half = FIRST * SUP
            for k, (arr, s) in enumerate(((src, src_loaded), (dst, dst_loaded))):
                sp.dma_start(raw[:, 2 * k, :], arr[0:half].rearrange("(s e) -> s e", e=SUP)).then_inc(s, 16)
                sp.dma_start(raw[0:SECOND - 1, 2 * k + 1, :],
                             arr[half:half + (SECOND - 1) * SUP].rearrange("(s e) -> s e", e=SUP)).then_inc(s, 16)
                sp.dma_start(raw[SECOND - 1:SECOND, 2 * k + 1, :],
                             arr[TAIL_START:EDGES].rearrange("(s e) -> s e", s=1)).then_inc(s, 16)
            sp.wait_ge(pad_cleared, 1)
            for g in range(GROUPS):
                b0, nb = g * GB, len(group_blocks(g))
                if g < GROUPS - 1:
                    sp.dma_start(rows_x[:, b0:b0 + nb, :],
                                 x[b0 * P:(b0 + nb) * P, :].rearrange("(b p) d -> p b d", p=P)).then_inc(x_loaded[g], 16)
                else:
                    sp.dma_start(rows_x[0:LAST_BLOCK, b0, :], x[b0 * P:NODES, :]).then_inc(x_loaded[g], 16)
            for l in range(2):
                sp.dma_start(w_first[:, l, :], W1[l]).then_inc(params_loaded, 16)
                sp.dma_start(w_second[:, l, :], W2[l]).then_inc(params_loaded, 16)
                for dst_col, a in ((bias_first[:, l:l + 1], b1), (bias_second[:, l:l + 1], b2),
                                   (bn_gamma[:, l:l + 1], gamma), (bn_beta[:, l:l + 1], beta)):
                    sp.dma_start(dst_col, a[l:l + 1, :].rearrange("o d -> d o")).then_inc(params_loaded, 16)
            for k, a in enumerate((w1a, w1b, w2a, w2b)):
                sp.dma_start(w_rows[:, k, :], a).then_inc(params_loaded, 16)
            for dst_col, a in ((bias_first[:, 2:3], b1a), (bias_second[:, 2:3], b1b),
                               (bias_first[:, 3:4], b2a), (bias_second[:, 3:4], b2b)):
                sp.dma_start(dst_col, a.rearrange("(d o) -> d o", o=1)).then_inc(params_loaded, 16)
            for k, a in enumerate((eps1, eps2)):
                sp.dma_start(eps_col[:, k:k + 1],
                             a.rearrange("(o e) -> o e", o=1).broadcast_to((P, 1))).then_inc(params_loaded, 16)

            def store_table(version):
                for g in range(GROUPS):
                    b0, nb = g * GB, len(group_blocks(g))
                    sp.wait_ge(rows_ready, version * LG + g + 1)
                    sp.dma_start(table_b[:, b0:b0 + nb, :], rows_h[:, b0:b0 + nb, :]).then_inc(table_written, 16)

            def load_supertile(u, n, first):
                sp.wait_ge(reduced[u], n)
                sp.dma_start(ea[:, u, :, :].rearrange("p j d -> p (j d)"),
                             edge_attr[bass.DynSlice(first, SUP), :].rearrange("(p j) d -> p (j d)", j=EPP)
                             ).then_inc(ea_loaded[u], 16)

            def load_edges(layer, rounds):
                with sp.Fori(0, rounds) as r:
                    before = turns_before(sp, rounds, layer, r)
                    with sp.Fori(0, TURNS - 1) as i:
                        n = sp.snap(before + i + 1)
                        for u in range(SLOTS):
                            load_supertile(u, n, (i * SLOTS + u) * SUP)
                    n = sp.snap(before + TURNS)
                    for u in range(SLOTS):
                        load_supertile(u, n, min(((TURNS - 1) * SLOTS + u) * SUP, TAIL_START))

            sp.wait_ge(rounds_ready, 1)
            rounds = sp.value_load(rounds_i[0:1, 0:1], min_val=1, max_val=BLOCKS)
            store_table(0)
            load_edges(0, rounds)
            store_table(1)
            load_edges(1, rounds)
            store_table(2)
            store_table(3)
            for g in range(GROUPS):
                b0, nb = g * GB, len(group_blocks(g))
                sp.wait_ge(rows_ready, LAYERS * LG + g + 1)
                if g < GROUPS - 1:
                    sp.dma_start(out[b0 * P:(b0 + nb) * P, :].rearrange("(b p) d -> p b d", p=P),
                                 rows_h[:, b0:b0 + nb, :]).then_inc(out_written, 16)
                else:
                    sp.dma_start(out[b0 * P:NODES, :], rows_h[0:LAST_BLOCK, b0, :]).then_inc(out_written, 16)
            sp.wait_ge(out_written, 16 * GROUPS)

        @block.gpsimd
        def _(pool):
            nc.gpsimd.memset(rows_x[:, BLOCKS - 1, :], 0.0).then_inc(pad_cleared, 1)
            nc.gpsimd.memset(acc[:, PADDED:ACC], 0.0).then_inc(consts_made, 1)
            nc.gpsimd.iota(iota0[:, :], pattern=[[1, WIN]], base=0, channel_multiplier=0,
                           allow_small_or_imprecise_dtypes=True).then_inc(consts_made, 1)
            nc.gpsimd.memset(small_eps[:, :], LN_EPS).then_inc(consts_made, 1)
            nc.gpsimd.memset(ident[:, :], 0.0).then_inc(consts_made, 1)
            pool.wait_ge(consts_made, 4)
            nc.gpsimd.affine_select(out=ident[:, :], in_=ident[:, :], compare_op=ALU.not_equal, fill=1.0,
                                    base=0, pattern=[[-1, P]], channel_multiplier=1).then_inc(consts_made, 1)
            pool.wait_ge(rounds_ready, 1)
            rounds = pool.value_load(rounds_i[0:1, 0:1], min_val=1, max_val=BLOCKS)
            for layer in range(LAYERS):
                pool.wait_ge(table_written, 16 * GROUPS * (layer + 1))
                with pool.Fori(0, rounds) as r:
                    before = turns_before(pool, rounds, layer, r)
                    with pool.Fori(0, TURNS) as i:
                        n = pool.snap(before + i + 1)
                        for u in range(SLOTS):
                            pool.wait_ge(idx_ready[u], n)
                            pool.wait_ge(summed[u] if layer < 2 else reduced[u], n)
                            pool.sem_inc(slots_opened, 1)
                            for j in range(EPP):
                                nc.gpsimd.indirect_dma_start(
                                    xg[:, u, j, :], None, table,
                                    bass.IndirectOffsetOnAxis(ap=idx[:, u, j:j + 1], axis=0),
                                ).then_inc(gathered[u][j], 16)

        @block.scalar
        def _(act):
            for half in range(2):
                rows = (FIRST, SECOND)[half]
                act.wait_ge(src_turned, half + 1)
                act.copy(src_all[:, half * FIRST:half * FIRST + rows, :].rearrange("p s j -> p j s"),
                         psG[:, half, :].rearrange("p (j s) -> p j s", j=EPP)[:, :, 0:rows]).then_inc(src_ready, 1)
            act.wait_ge(src_ready, 2)
            act.copy(src_all[:, SUPERS:SUPERS + SLOTS, :], src_all[:, 0:SLOTS, :]).then_inc(src_ready, 1)
            for u in range(SLOTS):
                act.copy(idx[:, u, :], src_all[:, u, :]).then_inc(idx_ready[u], 1)
            def norm_rows(q, version):
                act.wait_ge(ln_var_ready, q + 1)
                act.activation(ln_rstd[:, :], ln_mv[:, :, 1], ACT.Sqrt, bias=small_eps[:, 0:1]).then_inc(ln_std_ready, 1)
                if version > 0:
                    act.wait_ge(table_written, 16 * LG * version)
                for g in range(GROUPS):
                    b = slice(g * GB, g * GB + len(group_blocks(g)))
                    act.wait_ge(normed, q * LG + g + 1)
                    act.activation(rows_h[:, b, :], rows_h[:, b, :], ACT.Relu).then_inc(rows_ready, 1)
                    if g >= 2:
                        turn_out(q, g - 2)
                for g in range(GROUPS - 2, GROUPS):
                    turn_out(q, g)

            def turn_out(q, g):
                c0, w = group_cols(g)
                act.wait_ge(cols_turned, q * LG + g + 1)
                if q == 0:
                    act.copy(acc[:, c0:c0 + w], psG[:, g % 4, 0:w]).then_inc(cols_ready, 1)
                else:
                    act.activation(acc[:, c0:c0 + w], psG[:, g % 4, 0:w], ACT.Copy,
                                   scale=one_eps[:, 0:1]).then_inc(cols_ready, 1)

            def edges(layer, rounds):
                with act.Fori(0, rounds) as r:
                    before = turns_before(act, rounds, layer, r)
                    with act.Fori(0, TURNS) as i:
                        n = act.snap(before + i + 1)
                        nxt = act.snap(n + 1)
                        n16 = act.snap(n * 16)
                        for u in range(SLOTS):
                            if layer < 2:
                                act.wait_ge(summed[u], nxt)
                                act.activation(ea[:, u, :, :], ea[:, u, :, :], ACT.Relu).then_inc(msg_ready[u], 1)
                            else:
                                for j in range(EPP):
                                    act.wait_ge(gathered[u][j], n16)
                            s = act.snap(i * SLOTS + (u + SLOTS))
                            act.copy(idx[:, u, :], src_all[:, bass.DynSlice(s, 1), :].rearrange("p o j -> p (o j)")
                                     ).then_inc(idx_ready[u], 1)

            def mlp(layer):
                for g in range(GROUPS):
                    c0, w = group_cols(g)
                    act.wait_ge(first_done, layer * LG + g + 1)
                    act.activation(hid[:, c0:c0 + w], psG[:, g % 4, 0:w], ACT.Identity if layer < 2 else ACT.Relu,
                                   bias=bias_first[:, layer:layer + 1]).then_inc(hid_ready, 1)
                if layer < 2:
                    act.wait_ge(bn_var_ready, layer + 1)
                    act.activation(bn_std[:, :], bn_mv[:, 1:2], ACT.Sqrt, bias=small_eps[:, 0:1]).then_inc(bn_std_ready, 1)
                    act.wait_ge(bn_ready, layer + 1)
                    act.wait_ge(hid_ready, (layer + 1) * LG)
                    for g in range(GROUPS):
                        c0, w = group_cols(g)
                        act.activation(hid[:, c0:c0 + w], hid[:, c0:c0 + w], ACT.Relu, bias=bn_shift[:, 0:1],
                                       scale=bn_scale[:, 0:1]).then_inc(act_ready, 1)
                if layer in (0, 2):
                    version = (1, None, 3)[layer]
                    act.wait_ge(table_written, 16 * LG * version)
                    for g in range(GROUPS):
                        b0, nb = g * GB, len(group_blocks(g))
                        act.wait_ge(rows_turned, layer * LG + g + 1)
                        act.copy(rows_h[:, b0:b0 + nb, :], psG[:, g % 4, 0:nb * P].rearrange("p (b d) -> p b d", d=D)
                                 ).then_inc(rows_ready, 1)

            act.wait_ge(consts_made, 5)
            norm_rows(0, 0)
            act.wait_ge(weights_turned, 1)
            for k in range(4):
                dst_w = (w_first, w_second)[k % 2]
                act.copy(dst_w[:, 2 + k // 2, :], psG[:, 1, k * P:(k + 1) * P]).then_inc(weights_ready, 1)
            act.wait_ge(rounds_ready, 1)
            rounds = act.value_load(rounds_i[0:1, 0:1], min_val=1, max_val=BLOCKS)
            act.wait_ge(params_loaded, PARAMS)
            for layer in range(LAYERS):
                edges(layer, rounds)
                mlp(layer)
                if layer == 1:
                    norm_rows(1, 2)

        @block.vector
        def _(dve):
            steps = [0]

            def link(ins):
                steps[0] += 1
                ins.then_inc(vec, 1)
                dve.wait_ge(vec, steps[0])

            for u in range(SLOTS):
                dve.sem_inc(summed[u], 1)
                dve.sem_inc(added[u], 1)

            halves = ((0, FIRST), (1, SECOND))
            dve.wait_ge(src_loaded, 48)
            for h, rows in halves:
                nc.vector.tensor_copy(flt[0:rows, h, :], raw[0:rows, h, :]).then_inc(src_float, 1)
            dve.wait_ge(dst_loaded, 48)
            for h, rows in halves:
                f = flt[0:rows, 2 + h, :]
                st = win_stat[0:rows, h, :]
                link(nc.vector.tensor_copy(f, raw[0:rows, 2 + h, :]))
                link(nc.vector.tensor_reduce(st[:, 0:1], f, AX_X, ALU.min))
                link(nc.vector.tensor_reduce(st[:, 1:2], f, AX_X, ALU.max))
                nc.vector.tensor_tensor(st[:, 2:3], st[:, 1:2], st[:, 0:1], ALU.subtract).then_inc(stat_ready, 1)
                nc.vector.tensor_scalar(f, f, st[:, 0:1], None, ALU.subtract).then_inc(loc_float, 1)
            for h, rows in halves:
                dve.wait_ge(loc_turned, h + 1)
                nc.vector.tensor_copy(loc_all[:, h * FIRST:h * FIRST + rows, :].rearrange("p s j -> p j s"),
                                      psG[:, 2 + h, :].rearrange("p (j s) -> p j s", j=EPP)[:, :, 0:rows]
                                      ).then_inc(loc_ready, 1)
            dve.wait_ge(loc_ready, 2)
            link(nc.vector.memset(loc_all[0:OVERLAP // EPP, SUPERS - 1, :], -1.0))
            dve.wait_ge(base_turned, 1)
            nc.vector.tensor_copy(base_f[:, :], psW[0:1, 0, 0:SUPERS])
            link(nc.vector.tensor_reduce(spread_f[:, 0:1], psW[0:1, 1, 0:SUPERS], AX_X, ALU.max))
            link(nc.vector.tensor_scalar(spread_f[:, 1:2], spread_f[:, 0:1], float(WIN), None, ALU.add))
            link(nc.vector.tensor_copy(rounds_i[:, 1:2], spread_f[:, 1:2]))
            nc.vector.tensor_scalar(rounds_i[:, 0:1], rounds_i[:, 1:2], WIN.bit_length() - 1, None,
                                    ALU.arith_shift_right).then_inc(rounds_ready, 1)

            def norm_rows(q, version):
                for g in range(GROUPS):
                    if q == 0:
                        if g == 0:
                            dve.wait_ge(pad_cleared, 1)
                        dve.wait_ge(x_loaded[g], 16)
                    for b in group_blocks(g):
                        last = nc.vector.bn_stats(ln_stats[:, b, :], rows_x[:, b, :])
                link(last)
                for b in range(BLOCKS):
                    last = nc.vector.bn_aggr(ln_mv[:, b, :], ln_stats[:, b, :])
                last.then_inc(ln_var_ready, 1)
                dve.wait_ge(ln_std_ready, q + 1)
                link(nc.vector.reciprocal(ln_rstd[:, :], ln_rstd[:, :]))
                if version > 0:
                    dve.wait_ge(table_written, 16 * LG * version)
                for g in range(GROUPS):
                    for b in group_blocks(g):
                        last = nc.vector.tensor_scalar(rows_h[:, b, :], rows_x[:, b, :], ln_mv[:, b, 0:1],
                                                       ln_rstd[:, b:b + 1], ALU.subtract, ALU.mult)
                    last.then_inc(normed, 1)

            def edges(layer, rounds):
                link(nc.vector.tensor_copy(cur_base_f[:, :], base_f[:, :]))
                link(nc.vector.tensor_copy(cur_iota[:, :], iota0[:, :]))
                with dve.Fori(0, rounds) as r:
                    nc.vector.tensor_copy(cur_base[:, :], cur_base_f[:, :]).then_inc(round_step, 1)
                    passed = dve.snap((rounds * layer + r) * 3 + 1)
                    dve.wait_ge(round_step, passed)
                    dve.sem_inc(rounds_opened, 1)
                    before = turns_before(dve, rounds, layer, r)
                    with dve.Fori(0, TURNS) as i:
                        n = dve.snap(before + i + 1)
                        nxt = dve.snap(n + 1)
                        n16 = dve.snap(n * 16)

                        def add_window(u):
                            first = dve.value_load(cur_base[0:1, bass.DynSlice(i * SLOTS + u, 1)],
                                                   min_val=0, max_val=NODES)
                            dve.wait_ge(reduced[u], nxt)
                            dve.wait_ge(added[(u - 1) % SLOTS], nxt if u else n)
                            cols = acc[:, bass.DynSlice(first, WIN)]
                            nc.vector.tensor_tensor(cols, cols, psW[:, u, 0:WIN], ALU.add).then_inc(added[u], 1)

                        for u in range(SLOTS):
                            dve.wait_ge(reduced[u], n)
                            loc = loc_all[:, bass.DynSlice(i * SLOTS + u, 1), :].rearrange("p o j -> p (o j)")
                            nc.vector.tensor_tensor(
                                hot[:, u, :, :], cur_iota[:, :].unsqueeze(1).broadcast_to((P, EPP, WIN)),
                                loc.unsqueeze(2).broadcast_to((P, EPP, WIN)), ALU.is_equal).then_inc(hot_ready[u], 1)
                            if layer < 2:
                                for j in range(EPP):
                                    dve.wait_ge(gathered[u][j], n16)
                                dve.wait_ge(ea_loaded[u], n16)
                                nc.vector.tensor_tensor(ea[:, u, :, :], ea[:, u, :, :], xg[:, u, :, :],
                                                        ALU.add).then_inc(summed[u], 1)
                            if u > 0:
                                add_window(u - 1)
                        add_window(SLOTS - 1)
                    nc.vector.tensor_scalar(cur_base_f[:, :], cur_base_f[:, :], float(WIN), float(NODES),
                                            ALU.add, ALU.min).then_inc(round_step, 1)
                    nc.vector.tensor_scalar(cur_iota[:, :], cur_iota[:, :], float(WIN), None, ALU.add).then_inc(round_step, 1)
                    dve.wait_ge(round_step, dve.snap((rounds * layer + r) * 3 + 3))

            def mlp(layer, rounds):
                if layer < 2:
                    for g in range(GROUPS):
                        c0, _ = group_cols(g)
                        dve.wait_ge(hid_ready, layer * LG + g + 1)
                        last = nc.vector.bn_stats(bn_stats[:, g, :], hid[:, c0:c0 + real_cols(g)])
                    last.then_inc(bn_step, 1)
                    dve.wait_ge(bn_step, 4 * layer + 1)
                    nc.vector.bn_aggr(bn_mv[:, :], bn_stats[:, :, :].rearrange("p g k -> p (g k)")).then_inc(bn_var_ready, 1)
                    dve.wait_ge(bn_std_ready, layer + 1)
                    nc.vector.reciprocal(bn_tmp[:, :], bn_std[:, :]).then_inc(bn_step, 1)
                    dve.wait_ge(bn_step, 4 * layer + 2)
                    nc.vector.tensor_tensor(bn_scale[:, :], bn_tmp[:, :], bn_gamma[:, layer:layer + 1], ALU.mult).then_inc(bn_step, 1)
                    dve.wait_ge(bn_step, 4 * layer + 3)
                    nc.vector.tensor_tensor(bn_tmp[:, :], bn_mv[:, 0:1], bn_scale[:, :], ALU.mult).then_inc(bn_step, 1)
                    dve.wait_ge(bn_step, 4 * layer + 4)
                    nc.vector.tensor_tensor(bn_shift[:, :], bn_beta[:, layer:layer + 1], bn_tmp[:, :], ALU.subtract).then_inc(bn_ready, 1)
                for g in range(GROUPS):
                    c0, w = group_cols(g)
                    dve.wait_ge(second_done, layer * LG + g + 1)
                    b = bias_second[:, layer:layer + 1]
                    if layer < 3:
                        ins = nc.vector.tensor_scalar(acc[:, c0:c0 + w], psW[:, g % 4, 0:w], b, 0.0, ALU.add, ALU.max)
                    else:
                        ins = nc.vector.tensor_scalar(acc[:, c0:c0 + w], psW[:, g % 4, 0:w], b, None, ALU.add)
                    ins.then_inc(next_ready, 1)
                if layer == 1:
                    for g in range(GROUPS):
                        b0, nb = g * GB, len(group_blocks(g))
                        dve.wait_ge(rows_turned, layer * LG + g + 1)
                        nc.vector.tensor_tensor(rows_x[:, b0:b0 + nb, :], rows_x[:, b0:b0 + nb, :],
                                                psG[:, g % 4, 0:nb * P].rearrange("p (b d) -> p b d", d=D), ALU.add
                                                ).then_inc(resid_ready, 1)
                    dve.wait_ge(resid_ready, GROUPS)
                if layer == 2:
                    for g in range(GROUPS):
                        c0, w = group_cols(g)
                        dve.wait_ge(rows_turned, layer * LG + g + 1)
                        nc.vector.tensor_scalar(acc[:, c0:c0 + w], acc[:, c0:c0 + w], one_eps[:, 1:2], None,
                                                ALU.mult).then_inc(acc_scaled, 1)
                if layer == 3:
                    dve.wait_ge(table_written, 16 * LG * LAYERS)
                    for g in range(GROUPS):
                        b0, nb = g * GB, len(group_blocks(g))
                        dve.wait_ge(rows_turned, layer * LG + g + 1)
                        nc.vector.tensor_tensor(rows_h[:, b0:b0 + nb, :], rows_x[:, b0:b0 + nb, :],
                                                psG[:, g % 4, 0:nb * P].rearrange("p (b d) -> p b d", d=D), ALU.add
                                                ).then_inc(rows_ready, 1)

            norm_rows(0, 0)
            dve.wait_ge(params_loaded, PARAMS)
            for k in range(2):
                nc.vector.tensor_scalar(one_eps[:, k:k + 1], eps_col[:, k:k + 1], 1.0, None, ALU.add).then_inc(weights_ready, 1)
            dve.wait_ge(rounds_ready, 1)
            rounds = dve.value_load(rounds_i[0:1, 0:1], min_val=1, max_val=BLOCKS)
            for layer in range(LAYERS):
                if layer in (0, 2):
                    dve.wait_ge(cols_ready, (layer // 2 + 1) * LG)
                    dve.wait_ge(consts_made, 5)
                elif layer == 1:
                    dve.wait_ge(next_ready, 1 * LG)
                else:
                    dve.wait_ge(acc_scaled, LG)
                edges(layer, rounds)
                mlp(layer, rounds)
                if layer == 1:
                    norm_rows(1, 2)

        @block.tensor
        def _(pe):
            for u in range(SLOTS):
                pe.sem_inc(reduced[u], 1)
            pe.wait_ge(consts_made, 5)

            def turn_indices(tables, ready, bank0, done):
                for h, rows in ((0, FIRST), (1, SECOND)):
                    pe.wait_ge(ready, h + 1)
                    for j in range(EPP):
                        last = nc.tensor.transpose(psG[:, bank0 + h, j * P:j * P + rows],
                                                   flt[0:rows, tables + h, j::EPP], ident[0:rows, 0:rows])
                    last.then_inc(done, 1)

            turn_indices(0, src_float, 0, src_turned)
            turn_indices(2, loc_float, 2, loc_turned)
            pe.wait_ge(stat_ready, 2)
            for h, rows in ((0, FIRST), (1, SECOND)):
                for k, col in ((0, 0), (1, 2)):
                    last = nc.tensor.matmul(psW[0:1, k, h * FIRST:h * FIRST + rows], win_stat[0:rows, h, col:col + 1],
                                            ident[0:rows, 0:rows], start=(h == 0), stop=True, skip_group_check=True)
            last.then_inc(base_turned, 1)
            pe.wait_ge(loc_ready, 2)
            pe.wait_ge(src_ready, 2)

            def turn_rows(q):
                for g in range(GROUPS):
                    pe.wait_ge(rows_ready, (0, 2)[q] * LG + g + 1)
                    if g >= 4:
                        pe.wait_ge(cols_ready, q * LG + g - 3)
                    for k, b in enumerate(group_blocks(g)):
                        last = nc.tensor.transpose(psG[:, g % 4, k * P:(k + 1) * P], rows_h[:, b, :], ident[:, :])
                    last.then_inc(cols_turned, 1)

            def edges(layer, rounds):
                with pe.Fori(0, rounds) as r:
                    before = turns_before(pe, rounds, layer, r)
                    with pe.Fori(0, TURNS) as i:
                        n = pe.snap(before + i + 1)
                        n16 = pe.snap(n * 16)
                        for u in range(SLOTS):
                            pe.wait_ge(added[u], n)
                            pe.wait_ge(hot_ready[u], n)
                            if layer < 2:
                                pe.wait_ge(msg_ready[u], n)
                            for j in range(EPP):
                                if layer >= 2:
                                    pe.wait_ge(gathered[u][j], n16)
                                msg = ea if layer < 2 else xg
                                last = nc.tensor.matmul(psW[:, u, 0:WIN], msg[:, u, j, :], hot[:, u, j, :],
                                                        start=(j == 0), stop=(j == EPP - 1))
                            last.then_inc(reduced[u], 1)

            def mlp(layer, rounds):
                for u in range(SLOTS):
                    pe.wait_ge(added[u], pe.snap(rounds * ((layer + 1) * TURNS) + 1))
                for g in range(GROUPS):
                    c0, w = group_cols(g)
                    if g >= 4:
                        pe.wait_ge(hid_ready, layer * LG + g - 3)
                    nc.tensor.matmul(psG[:, g % 4, 0:w], w_first[:, layer, :], acc[:, c0:c0 + w],
                                     start=True, stop=True).then_inc(first_done, 1)
                for g in range(GROUPS):
                    c0, w = group_cols(g)
                    pe.wait_ge(act_ready if layer < 2 else hid_ready, layer * LG + g + 1)
                    if g >= 4:
                        pe.wait_ge(next_ready, layer * LG + g - 3)
                    nc.tensor.matmul(psW[:, g % 4, 0:w], w_second[:, layer, :], hid[:, c0:c0 + w],
                                     start=True, stop=True).then_inc(second_done, 1)
                for g in range(GROUPS):
                    pe.wait_ge(next_ready, layer * LG + g + 1)
                    if g >= 4:
                        pe.wait_ge({0: rows_ready, 1: resid_ready, 2: rows_ready, 3: rows_ready}[layer],
                                   {0: 1, 1: 0, 2: 3, 3: 4}[layer] * LG + g - 3)
                    elif layer >= 2:
                        pe.wait_ge(hid_ready, (layer + 1) * LG)
                    for k, b in enumerate(group_blocks(g)):
                        last = nc.tensor.transpose(psG[:, g % 4, k * P:(k + 1) * P], acc[:, b * P:(b + 1) * P], ident[:, :])
                    last.then_inc(rows_turned, 1)

            turn_rows(0)
            pe.wait_ge(params_loaded, PARAMS)
            pe.wait_ge(cols_ready, LG)
            for k in range(4):
                last = nc.tensor.transpose(psG[:, 1, k * P:(k + 1) * P], w_rows[:, k, :], ident[:, :])
            last.then_inc(weights_turned, 1)
            pe.wait_ge(weights_ready, 6)
            pe.wait_ge(rounds_ready, 1)
            rounds = pe.value_load(rounds_i[0:1, 0:1], min_val=1, max_val=BLOCKS)
            for layer in range(LAYERS):
                edges(layer, rounds)
                mlp(layer, rounds)
                if layer == 1:
                    turn_rows(1)


_INS = ['x', 'src', 'dst', 'edge_attr_128', 'L0_gnn_W1', 'L0_gnn_b1', 'L0_gnn_gamma', 'L0_gnn_beta', 'L0_gnn_W2',
        'L0_gnn_b2', 'L1_gnn_w1a', 'L1_gnn_b1a', 'L1_gnn_w1b', 'L1_gnn_b1b', 'L1_gnn_eps1', 'L1_gnn_w2a',
        'L1_gnn_b2a', 'L1_gnn_w2b', 'L1_gnn_b2b', 'L1_gnn_eps2']


def kernel(**inputs):
    import numpy as _np
    import concourse.bacc as _bacc
    from concourse import mybir as _mybir
    from concourse.bass_utils import run_bass_kernel_spmd as _run

    nc = _bacc.Bacc("TRN2", target_bir_lowering=False, num_devices=1)
    arrays, args = {}, []
    for name in _INS:
        a = _np.ascontiguousarray(_np.atleast_1d(_np.asarray(inputs[name])))
        arrays[f"in_{name}_dram"] = a
        args.append(nc.dram_tensor(f"in_{name}_dram", a.shape, _mybir.dt.from_np(a.dtype), kind="ExternalInput").ap())
    out = nc.dram_tensor("out_dram", (NODES, D), F32, kind="ExternalOutput").ap()
    gnn_kernel(nc, *args, out)
    r = _run(nc, [arrays], core_ids=[0])
    return r.results[0]["out_dram"]
```

```python
from contextlib import ExitStack

import concourse.bass as bass
from concourse import mybir

ALU = mybir.AluOpType
ACT = mybir.ActivationFunctionType
AX_X = mybir.AxisListType.X
F32 = mybir.dt.float32
I32 = mybir.dt.int32
I16 = mybir.dt.int16
F16 = mybir.dt.float16
BF16 = mybir.dt.bfloat16

P = 128
NODES = 6250
EDGES = 100000
D = 128
EPP = 4
SUP = P * EPP
SUPERS = -(-EDGES // SUP)
TAIL_START = EDGES - SUP
OVERLAP = SUPERS * SUP - EDGES
SLOTS = 4
TURNS = SUPERS // SLOTS
WIN = 128
BLOCKS = -(-NODES // P)
PADDED = BLOCKS * P
ACC = PADDED + WIN
GB = 4
GROUPS = -(-BLOCKS // GB)
FIRST = P
SECOND = SUPERS - FIRST
LAST_BLOCK = NODES - (BLOCKS - 1) * P
CW = 36
CB = BLOCKS * CW
CBANK = 512 // CW
BUILDS = 2 * TURNS
SKIP = TURNS // 2
COUNTED = SKIP * SLOTS
KEPT = (TURNS - SKIP) * SLOTS
HALF_B = BLOCKS // 2
PARTS = 3
LN_EPS = 1e-5
BN_EPS = 1e-5
LAYERS = 4

assert SUPERS % SLOTS == 0 and OVERLAP % EPP == 0 and SECOND <= P
assert COUNTED <= BUILDS <= KEPT and -(-BLOCKS // CBANK) <= 4 and SKIP <= FIRST


def group_blocks(g):
    return range(g * GB, min((g + 1) * GB, BLOCKS))


def group_cols(g):
    return g * GB * P, len(group_blocks(g)) * P


def real_cols(g):
    c0, n = group_cols(g)
    return min(n, NODES - c0)


def gnn_kernel(nc, x, src, dst, edge_attr, W1, b1, gamma, beta, W2, b2,
               w1a, b1a, w1b, b1b, eps1, w2a, b2a, w2b, b2b, eps2, out):
    with ExitStack() as ctx:
        ctx.enter_context(nc.allow_non_contiguous_dma(reason="columns of biases"))

        def sb(name, shape, dt=F32):
            return ctx.enter_context(nc.sbuf_tensor(name, shape, dt))

        def sem(name):
            return ctx.enter_context(nc.semaphore(name))

        count_store = nc.dram_tensor("count_store", [KEPT, P, CB], F16, kind="Internal").ap()
        table = nc.dram_tensor("node_table", [PADDED, D], F32, kind="Internal").ap()

        ident = sb("ident", [P, P])
        iota0 = sb("iota0", [P, WIN])
        iota_c = sb("iota_c", [P, CB], I16)
        round_off = sb("round_off", [P, BLOCKS])
        ones_row = sb("ones_row", [1, P])
        w_first = sb("w_first", [P, LAYERS, D])
        w_second = sb("w_second", [P, LAYERS, D])
        w_rows = sb("w_rows", [P, 4, D])
        bias_first = sb("bias_first", [P, LAYERS])
        bias_second = sb("bias_second", [P, LAYERS])
        bn_gamma = sb("bn_gamma", [P, 2])
        bn_beta = sb("bn_beta", [P, 2])
        eps_col = sb("eps_col", [P, 2])
        one_eps = sb("one_eps", [P, 2])
        small_eps = sb("small_eps", [P, 1])
        hid = sb("hid", [P, PADDED])
        raw = hid[:, 0:4 * SUP].bitcast(I32).rearrange("p (t e) -> p t e", t=4)
        flt = hid[:, 4 * SUP:8 * SUP].rearrange("p (t e) -> p t e", t=4)
        src_hi = hid[:, 8 * SUP:8 * SUP + COUNTED * EPP].bitcast(I32).rearrange("p (s j) -> p s j", j=EPP)
        src_lo = hid[:, 9 * SUP:9 * SUP + BUILDS * EPP].bitcast(I32).rearrange("p (s j) -> p s j", j=EPP)
        win_stat = sb("win_stat", [P, 2, 3])
        src_all = sb("src_all", [P, SUPERS + SLOTS, EPP], I32)
        loc_all = sb("loc_all", [P, SUPERS, EPP])
        base_f = sb("base_f", [1, SUPERS])
        base_i = sb("base_i", [1, SUPERS], I32)
        plan_f = sb("plan_f", [1, 8])
        rounds_t = sb("rounds_t", [1, 1], I32)
        plan_i = sb("plan_i", [1, 4], I32)
        use_counts = sb("use_counts", [P, 1])
        cell_all = sb("cell_all", [P, BUILDS, EPP])
        src_lo_all = sb("src_lo_all", [P, BUILDS, EPP])
        rows_x = sb("rows_x", [P, BLOCKS, D])
        rows_h = sb("rows_h", [P, BLOCKS, D])
        acc = sb("acc", [P, ACC])
        hid_rows = hid[:, :].rearrange("p (b d) -> p b d", d=D)
        ln_stats = sb("ln_stats", [P, BLOCKS, 6])
        ln_mv = sb("ln_mv", [P, BLOCKS, 2])
        ln_rstd = sb("ln_rstd", [P, BLOCKS])
        bn_stats = sb("bn_stats", [P, GROUPS, 6])
        bn_mv = sb("bn_mv", [P, 2])
        bn_std = sb("bn_std", [P, 1])
        bn_scale = sb("bn_scale", [P, 1])
        bn_shift = sb("bn_shift", [P, 1])
        bn_tmp = sb("bn_tmp", [P, 1])
        idx = sb("idx", [P, SLOTS, EPP], I32)
        xg = sb("xg", [P, SLOTS, EPP, D])
        ea = sb("ea", [P, SLOTS, EPP, D])
        hot = sb("hot", [P, SLOTS, EPP, WIN])
        first_i = sb("first_i", [1, SLOTS], I32)
        cells = sb("cells", [P, SLOTS, CB], F16)
        counts = cells
        src_hot = sb("src_hot", [P, EPP, P], F16)
        product = sb("product", [P, SLOTS, CW])
        count_out = sb("count_out", [P, CB], F16)
        xp = sb("xp", [P, BLOCKS, PARTS, D], BF16)

        psG = ctx.enter_context(nc.psum_tensor("psG", [P, 4, 512], F32))
        psA = ctx.enter_context(nc.psum_tensor("psA", [P, 4, 512], F32))

        params_loaded = sem("params_loaded")
        x_loaded = [sem(f"x_loaded{g}") for g in range(GROUPS)]
        src_loaded = sem("src_loaded")
        dst_loaded = sem("dst_loaded")
        consts_made = sem("consts_made")
        pad_cleared = sem("pad_cleared")
        weights_turned = sem("weights_turned")
        weights_ready = sem("weights_ready")
        src_float = sem("src_float")
        src_turned = sem("src_turned")
        src_ready = sem("src_ready")
        loc_float = sem("loc_float")
        loc_turned = sem("loc_turned")
        loc_ready = sem("loc_ready")
        stat_ready = sem("stat_ready")
        base_turned = sem("base_turned")
        spread_ready = sem("spread_ready")
        flag_turned = sem("flag_turned")
        flag_ready = sem("flag_ready")
        split_ready = sem("split_ready")
        cells_planned = sem("cells_planned")
        zeros_made = sem("zeros_made")
        more_consts = sem("more_consts")
        plan_ready = sem("plan_ready")
        vec = sem("vec")
        ln_var_ready = sem("ln_var_ready")
        ln_std_ready = sem("ln_std_ready")
        normed = sem("normed")
        rows_ready = sem("rows_ready")
        table_written = sem("table_written")
        cols_turned = sem("cols_turned")
        cols_ready = sem("cols_ready")
        first_done = sem("first_done")
        hid_ready = sem("hid_ready")
        bn_var_ready = sem("bn_var_ready")
        bn_std_ready = sem("bn_std_ready")
        bn_ready = sem("bn_ready")
        act_ready = sem("act_ready")
        second_done = sem("second_done")
        next_ready = sem("next_ready")
        rows_turned = sem("rows_turned")
        acc_scaled = sem("acc_scaled")
        resid_ready = sem("resid_ready")
        hi_ready = sem("hi_ready")
        rest_ready = sem("rest_ready")
        mid_ready = sem("mid_ready")
        parts_ready = sem("parts_ready")
        firsts_ready = sem("firsts_ready")
        slots_opened = sem("slots_opened")
        bn_step = sem("bn_step")
        out_written = sem("out_written")

        idx_ready = [sem(f"idx_ready{u}") for u in range(SLOTS)]
        gathered = [[sem(f"gathered{u}_{j}") for j in range(EPP)] for u in range(SLOTS)]
        ea_loaded = [sem(f"ea_loaded{u}") for u in range(SLOTS)]
        cells_ready = sem("cells_ready")
        count_stored = sem("count_stored")
        counts_loaded = [sem(f"counts_loaded{h}") for h in range(2)]
        summed = [sem(f"summed{u}") for u in range(SLOTS)]
        reduced = [sem(f"reduced{u}") for u in range(SLOTS)]
        added = [sem(f"added{u}") for u in range(SLOTS)]
        counted = sem("counted")
        count_evicted = sem("count_evicted")
        counts_used = [sem(f"counts_used{h}") for h in range(2)]
        products_out = sem("products_out")
        counts_added = sem("counts_added")
        msg_ready = [sem(f"msg_ready{u}") for u in range(SLOTS)]
        hot_ready = [sem(f"hot_ready{u}") for u in range(SLOTS)]

        table_b = table.rearrange("(b p) d -> p b d", p=P)
        LG = GROUPS
        PARAMS = 16 * (2 * 6 + 4 + 4 + 2)

        SPLIT = [(0, 12), (12, 24), (24, 36), (36, BLOCKS)]
        NSPLIT = len(SPLIT)

        def load_plan(eng):
            eng.wait_ge(plan_ready, 3)
            return (eng.value_load(plan_i[0:1, 0:1], min_val=1, max_val=BLOCKS),
                    eng.value_load(plan_i[0:1, 1:2], min_val=0, max_val=SKIP),
                    eng.value_load(plan_i[0:1, 2:3], min_val=TURNS - SKIP, max_val=TURNS),
                    eng.value_load(plan_i[0:1, 3:4], min_val=0, max_val=1))

        def turns_before(layer, left):
            return layer * TURNS if layer < 2 else 2 * TURNS + (layer - 2) * left

        def turns_of(layer, left):
            return TURNS if layer < 2 else left

        block = ctx.enter_context(nc.Block())

        @block.sync
        def _(sp):
            half = FIRST * SUP
            for k, (arr, s) in enumerate(((src, src_loaded), (dst, dst_loaded))):
                sp.dma_start(raw[:, 2 * k, :], arr[0:half].rearrange("(s e) -> s e", e=SUP)).then_inc(s, 16)
                sp.dma_start(raw[0:SECOND - 1, 2 * k + 1, :],
                             arr[half:half + (SECOND - 1) * SUP].rearrange("(s e) -> s e", e=SUP)).then_inc(s, 16)
                sp.dma_start(raw[SECOND - 1:SECOND, 2 * k + 1, :],
                             arr[TAIL_START:EDGES].rearrange("(s e) -> s e", s=1)).then_inc(s, 16)
            sp.wait_ge(pad_cleared, 1)
            for g in range(GROUPS):
                b0, nb = g * GB, len(group_blocks(g))
                if g < GROUPS - 1:
                    sp.dma_start(rows_x[:, b0:b0 + nb, :],
                                 x[b0 * P:(b0 + nb) * P, :].rearrange("(b p) d -> p b d", p=P)).then_inc(x_loaded[g], 16)
                else:
                    sp.dma_start(rows_x[0:LAST_BLOCK, b0, :], x[b0 * P:NODES, :]).then_inc(x_loaded[g], 16)
            for l in range(2):
                sp.dma_start(w_first[:, l, :], W1[l]).then_inc(params_loaded, 16)
                sp.dma_start(w_second[:, l, :], W2[l]).then_inc(params_loaded, 16)
                for dst_col, a in ((bias_first[:, l:l + 1], b1), (bias_second[:, l:l + 1], b2),
                                   (bn_gamma[:, l:l + 1], gamma), (bn_beta[:, l:l + 1], beta)):
                    sp.dma_start(dst_col, a[l:l + 1, :].rearrange("o d -> d o")).then_inc(params_loaded, 16)
            for k, a in enumerate((w1a, w1b, w2a, w2b)):
                sp.dma_start(w_rows[:, k, :], a).then_inc(params_loaded, 16)
            for dst_col, a in ((bias_first[:, 2:3], b1a), (bias_second[:, 2:3], b1b),
                               (bias_first[:, 3:4], b2a), (bias_second[:, 3:4], b2b)):
                sp.dma_start(dst_col, a.rearrange("(d o) -> d o", o=1)).then_inc(params_loaded, 16)
            for k, a in enumerate((eps1, eps2)):
                sp.dma_start(eps_col[:, k:k + 1],
                             a.rearrange("(o e) -> o e", o=1).broadcast_to((P, 1))).then_inc(params_loaded, 16)

            def store_table(version):
                for g in range(GROUPS):
                    b0, nb = g * GB, len(group_blocks(g))
                    sp.wait_ge(rows_ready, version * LG + g + 1)
                    sp.dma_start(table_b[:, b0:b0 + nb, :], rows_h[:, b0:b0 + nb, :]).then_inc(table_written, 16)

            sp.wait_ge(zeros_made, 1)
            for a in range(BUILDS, KEPT):
                sp.dma_start(count_store[a], count_out[:, :]).then_inc(count_stored, 16)
            rounds, skipped, left, use = load_plan(sp)

            def load_supertile(u, last_use, first):
                sp.wait_ge(reduced[u], last_use)
                sp.dma_start(ea[:, u, :, :].rearrange("p j d -> p (j d)"),
                             edge_attr[bass.DynSlice(first, SUP), :].rearrange("(p j) d -> p (j d)", j=EPP)
                             ).then_inc(ea_loaded[u], 16)

            def store_counts(layer, k):
                sp.wait_ge(count_evicted, sp.snap(layer * TURNS + k + 2))
                sp.dma_start(count_store[bass.DynSlice(layer * TURNS + k, 1)].rearrange("o p c -> (o p) c"),
                             count_out[:, :]).then_inc(count_stored, 16)

            def load_edges(layer):
                with sp.Fori(0, TURNS - 1) as k:
                    last_use = sp.snap((k + layer * TURNS) * rounds + 1)
                    for u in range(SLOTS):
                        load_supertile(u, last_use, (k * SLOTS + u) * SUP)
                    store_counts(layer, k)
                last_use = sp.snap(rounds * ((layer + 1) * TURNS - 1) + 1)
                for u in range(SLOTS):
                    load_supertile(u, last_use, min(((TURNS - 1) * SLOTS + u) * SUP, TAIL_START))
                sp.wait_ge(count_evicted, (layer + 1) * TURNS + 1)
                sp.dma_start(count_store[(layer + 1) * TURNS - 1], count_out[:, :]).then_inc(count_stored, 16)

            def load_counts(layer):
                with sp.Fori(0, left) as k:
                    group = sp.snap(k * use).with_bounds(min_val=0, max_val=TURNS - SKIP - 1)
                    n = sp.snap(k + (layer - 2) * left + 1)
                    for h, b in ((0, slice(0, HALF_B * CW)), (1, slice(HALF_B * CW, CB))):
                        sp.wait_ge(counts_used[h], n)
                        sp.dma_start(counts[:, :, b],
                                     count_store[bass.DynSlice(group * SLOTS, SLOTS), :, b].rearrange("s p c -> p s c")
                                     ).then_inc(counts_loaded[h], 16)

            store_table(0)
            load_edges(0)
            store_table(1)
            load_edges(1)
            store_table(2)
            sp.wait_ge(counted, 2 * TURNS + 1)
            sp.wait_ge(count_stored, 16 * KEPT)
            load_counts(2)
            store_table(3)
            load_counts(3)
            for g in range(GROUPS):
                b0, nb = g * GB, len(group_blocks(g))
                sp.wait_ge(rows_ready, LAYERS * LG + g + 1)
                if g < GROUPS - 1:
                    sp.dma_start(out[b0 * P:(b0 + nb) * P, :].rearrange("(b p) d -> p b d", p=P),
                                 rows_h[:, b0:b0 + nb, :]).then_inc(out_written, 16)
                else:
                    sp.dma_start(out[b0 * P:NODES, :], rows_h[0:LAST_BLOCK, b0, :]).then_inc(out_written, 16)
            sp.wait_ge(out_written, 16 * GROUPS)

        @block.gpsimd
        def _(pool):
            nc.gpsimd.memset(rows_x[:, BLOCKS - 1, :], 0.0).then_inc(pad_cleared, 1)
            nc.gpsimd.memset(acc[:, PADDED:ACC], 0.0).then_inc(consts_made, 1)
            nc.gpsimd.iota(iota0[:, :], pattern=[[1, WIN]], base=0, channel_multiplier=0,
                           allow_small_or_imprecise_dtypes=True).then_inc(consts_made, 1)
            nc.gpsimd.memset(small_eps[:, :], LN_EPS).then_inc(consts_made, 1)
            nc.gpsimd.memset(ident[:, :], 0.0).then_inc(consts_made, 1)
            pool.wait_ge(consts_made, 4)
            nc.gpsimd.affine_select(out=ident[:, :], in_=ident[:, :], compare_op=ALU.not_equal, fill=1.0,
                                    base=0, pattern=[[-1, P]], channel_multiplier=1).then_inc(consts_made, 1)
            nc.gpsimd.iota(iota_c[:, :], pattern=[[1, CB]], base=0, channel_multiplier=0).then_inc(more_consts, 1)
            nc.gpsimd.iota(round_off[:, :], pattern=[[WIN, BLOCKS]], base=0, channel_multiplier=0,
                           allow_small_or_imprecise_dtypes=True).then_inc(more_consts, 1)
            nc.gpsimd.memset(ones_row[:, :], 1.0).then_inc(more_consts, 1)
            nc.gpsimd.memset(count_out[:, :], 0.0).then_inc(zeros_made, 1)
            rounds, skipped, left, use = load_plan(pool)
            for layer in range(LAYERS):
                pool.wait_ge(table_written, 16 * GROUPS * (layer + 1))
                before = turns_before(layer, left)
                with pool.Fori(0, turns_of(layer, left)) as k:
                    n = pool.snap(k + before + 1)
                    freed = n if layer < 2 else pool.snap((k + before) * rounds + 1)
                    for u in range(SLOTS):
                        pool.wait_ge(idx_ready[u], n)
                        pool.wait_ge(summed[u] if layer < 2 else reduced[u], freed)
                        pool.sem_inc(slots_opened, 1)
                        for j in range(EPP):
                            nc.gpsimd.indirect_dma_start(
                                xg[:, u, j, :], None, table,
                                bass.IndirectOffsetOnAxis(ap=idx[:, u, j:j + 1], axis=0),
                            ).then_inc(gathered[u][j], 16)

        @block.scalar
        def _(act):
            act.sem_inc(count_evicted, 1)
            act.sem_inc(products_out, 1)
            for half in range(2):
                rows = (FIRST, SECOND)[half]
                act.wait_ge(src_turned, half + 1)
                act.copy(src_all[:, half * FIRST:half * FIRST + rows, :].rearrange("p s j -> p j s"),
                         psG[:, half, :].rearrange("p (j s) -> p j s", j=EPP)[:, :, 0:rows]).then_inc(src_ready, 1)
            act.wait_ge(src_ready, 2)
            act.copy(src_all[:, SUPERS:SUPERS + SLOTS, :], src_all[:, 0:SLOTS, :]).then_inc(src_ready, 1)
            for u in range(SLOTS):
                act.copy(idx[:, u, :], src_all[:, u, :]).then_inc(idx_ready[u], 1)
            def norm_rows(q, version):
                act.wait_ge(ln_var_ready, q + 1)
                act.activation(ln_rstd[:, :], ln_mv[:, :, 1], ACT.Sqrt, bias=small_eps[:, 0:1]).then_inc(ln_std_ready, 1)
                if version > 0:
                    act.wait_ge(table_written, 16 * LG * version)
                for g in range(GROUPS):
                    b = slice(g * GB, g * GB + len(group_blocks(g)))
                    act.wait_ge(normed, q * LG + g + 1)
                    act.activation(rows_h[:, b, :], rows_h[:, b, :], ACT.Relu).then_inc(rows_ready, 1)
                    if g >= 2:
                        turn_out(q, g - 2)
                for g in range(GROUPS - 2, GROUPS):
                    turn_out(q, g)

            def turn_out(q, g):
                c0, w = group_cols(g)
                act.wait_ge(cols_turned, q * LG + g + 1)
                if q == 0:
                    act.copy(acc[:, c0:c0 + w], psG[:, g % 4, 0:w]).then_inc(cols_ready, 1)
                else:
                    act.activation(acc[:, c0:c0 + w], psG[:, g % 4, 0:w], ACT.Copy,
                                   scale=one_eps[:, 0:1]).then_inc(cols_ready, 1)

            def edges(layer):
                if layer == 1:
                    for u in range(SLOTS):
                        act.wait_ge(idx_ready[u], TURNS + 1)
                    act.copy(src_all[:, SUPERS:SUPERS + SLOTS, :],
                             src_all[:, bass.DynSlice((skipped * SLOTS), SLOTS), :]).then_inc(src_ready, 1)
                    act.wait_ge(src_ready, 4)
                with act.Fori(0, turns_of(layer, left)) as k:
                    before = turns_before(layer, left)
                    n = act.snap(k + before + 1)
                    if layer < 2:
                        nxt = act.snap(n + 1)
                    else:
                        n16 = act.snap(n * 16)
                        m = (layer - 2) * left + k + 1
                        act.wait_ge(counts_used[1], act.snap(m + 1))
                        act.wait_ge(counts_added, act.snap((m - 1) * SLOTS + 1))
                        act.copy(product[:, :, :], psA[:, 0, 0:SLOTS * CW].rearrange("p (s c) -> p s c", s=SLOTS)
                                 ).then_inc(products_out, 1)
                    first = 0 if layer < 2 else skipped * SLOTS
                    for u in range(SLOTS):
                        if layer < 2:
                            act.wait_ge(summed[u], nxt)
                        else:
                            for j in range(EPP):
                                act.wait_ge(gathered[u][j], n16)
                        s = act.snap(k * SLOTS + (u + SLOTS) + first).with_bounds(min_val=0, max_val=SUPERS + SLOTS - 1)
                        act.copy(idx[:, u, :], src_all[:, bass.DynSlice(s, 1), :].rearrange("p o j -> p (o j)")
                                 ).then_inc(idx_ready[u], 1)
                        if layer < 2:
                            act.activation(ea[:, u, :, :], ea[:, u, :, :], ACT.Relu).then_inc(msg_ready[u], 1)
                    if layer < 2:
                        act.wait_ge(counted, nxt)
                        act.wait_ge(count_stored, act.snap(n * 16 + 16 * (KEPT - BUILDS - 1)))
                        act.copy(count_out[:, 0:3 * CBANK * CW].rearrange("p (k c) -> p k c", k=3),
                                 psA[:, 0:3, 0:CBANK * CW])
                        act.copy(count_out[:, 3 * CBANK * CW:CB], psA[:, 3, 0:CB - 3 * CBANK * CW]).then_inc(count_evicted, 1)

            def split_features(layer):
                for c, (a, b) in enumerate(SPLIT):
                    act.wait_ge(rows_ready, (layer + 1) * LG)
                    act.activation(xp[:, a:b, 0, :], rows_h[:, a:b, :], ACT.Copy, scale=use_counts[:, 0:1]).then_inc(hi_ready, 1)
                for c, (a, b) in enumerate(SPLIT):
                    act.wait_ge(rest_ready, (layer - 2) * NSPLIT + c + 1)
                    act.copy(xp[:, a:b, 1, :], hid_rows[:, a:b, :]).then_inc(mid_ready, 1)

            def mlp(layer):
                for g in range(GROUPS):
                    c0, w = group_cols(g)
                    act.wait_ge(first_done, layer * LG + g + 1)
                    act.activation(hid[:, c0:c0 + w], psG[:, g % 4, 0:w], ACT.Identity if layer < 2 else ACT.Relu,
                                   bias=bias_first[:, layer:layer + 1]).then_inc(hid_ready, 1)
                if layer < 2:
                    act.wait_ge(bn_var_ready, layer + 1)
                    act.activation(bn_std[:, :], bn_mv[:, 1:2], ACT.Sqrt, bias=small_eps[:, 0:1]).then_inc(bn_std_ready, 1)
                    act.wait_ge(bn_ready, layer + 1)
                    act.wait_ge(hid_ready, (layer + 1) * LG)
                    for g in range(GROUPS):
                        c0, w = group_cols(g)
                        act.activation(hid[:, c0:c0 + w], hid[:, c0:c0 + w], ACT.Relu, bias=bn_shift[:, 0:1],
                                       scale=bn_scale[:, 0:1]).then_inc(act_ready, 1)
                if layer in (0, 2):
                    version = (1, None, 3)[layer]
                    act.wait_ge(table_written, 16 * LG * version)
                    for g in range(GROUPS):
                        b0, nb = g * GB, len(group_blocks(g))
                        act.wait_ge(rows_turned, layer * LG + g + 1)
                        act.copy(rows_h[:, b0:b0 + nb, :], psG[:, g % 4, 0:nb * P].rearrange("p (b d) -> p b d", d=D)
                                 ).then_inc(rows_ready, 1)

            act.wait_ge(consts_made, 5)
            norm_rows(0, 0)
            act.wait_ge(weights_turned, 1)
            for k in range(4):
                dst_w = (w_first, w_second)[k % 2]
                act.copy(dst_w[:, 2 + k // 2, :], psG[:, 1, k * P:(k + 1) * P]).then_inc(weights_ready, 1)
            rounds, skipped, left, use = load_plan(act)
            act.wait_ge(params_loaded, PARAMS)
            for layer in range(LAYERS):
                if layer >= 2:
                    split_features(layer)
                edges(layer)
                mlp(layer)
                if layer == 1:
                    norm_rows(1, 2)

        @block.vector
        def _(dve):
            steps = [0]

            def link(ins):
                steps[0] += 1
                ins.then_inc(vec, 1)
                dve.wait_ge(vec, steps[0])

            for u in range(SLOTS):
                dve.sem_inc(summed[u], 1)
                dve.sem_inc(added[u], 1)
            dve.sem_inc(counts_added, 1)

            halves = ((0, FIRST), (1, SECOND))
            dve.wait_ge(src_loaded, 48)
            for h, rows in halves:
                nc.vector.tensor_copy(flt[0:rows, h, :], raw[0:rows, h, :]).then_inc(src_float, 1)
            dve.wait_ge(dst_loaded, 48)
            for h, rows in halves:
                f = flt[0:rows, 2 + h, :]
                st = win_stat[0:rows, h, :]
                link(nc.vector.tensor_copy(f, raw[0:rows, 2 + h, :]))
                link(nc.vector.tensor_reduce(st[:, 0:1], f, AX_X, ALU.min))
                link(nc.vector.tensor_reduce(st[:, 1:2], f, AX_X, ALU.max))
                nc.vector.tensor_tensor(st[:, 2:3], st[:, 1:2], st[:, 0:1], ALU.subtract).then_inc(stat_ready, 1)
                nc.vector.tensor_scalar(f, f, st[:, 0:1], None, ALU.subtract).then_inc(loc_float, 1)
            for h, rows in halves:
                dve.wait_ge(loc_turned, h + 1)
                nc.vector.tensor_copy(loc_all[:, h * FIRST:h * FIRST + rows, :].rearrange("p s j -> p j s"),
                                      psG[:, 2 + h, :].rearrange("p (j s) -> p j s", j=EPP)[:, :, 0:rows]
                                      ).then_inc(loc_ready, 1)
            dve.wait_ge(loc_ready, 2)
            link(nc.vector.memset(loc_all[0:OVERLAP // EPP, SUPERS - 1, :], -1.0))
            dve.wait_ge(base_turned, 1)
            link(nc.vector.tensor_copy(base_i[:, :], psA[0:1, 0, 0:SUPERS]))
            link(nc.vector.tensor_copy(base_f[:, :], psA[0:1, 0, 0:SUPERS]))
            link(nc.vector.tensor_reduce(plan_f[:, 0:1], psA[0:1, 1, 0:SUPERS], AX_X, ALU.max))
            link(nc.vector.tensor_scalar(plan_f[:, 1:2], plan_f[:, 0:1], float(WIN), None, ALU.add))
            link(nc.vector.tensor_copy(rounds_t[:, :], plan_f[:, 1:2]))
            nc.vector.tensor_scalar(plan_i[:, 0:1], rounds_t[:, :], WIN.bit_length() - 1, None,
                                    ALU.arith_shift_right).then_inc(plan_ready, 1)
            link(nc.vector.tensor_reduce(plan_f[:, 2:3], psA[0:1, 1, 0:COUNTED], AX_X, ALU.max))
            nc.vector.tensor_scalar(plan_f[:, 3:4], plan_f[:, 2:3], float(CW), None, ALU.is_lt).then_inc(flag_ready, 1)
            dve.wait_ge(flag_ready, 1)
            nc.vector.tensor_copy(plan_i[:, 3:4], plan_f[:, 3:4])
            nc.vector.tensor_scalar(plan_i[:, 1:2], plan_f[:, 3:4], float(SKIP), None, ALU.mult).then_inc(plan_ready, 1)
            nc.vector.tensor_scalar(plan_i[:, 2:3], plan_f[:, 3:4], -float(SKIP), float(TURNS), ALU.mult,
                                    ALU.add).then_inc(plan_ready, 1)
            dve.wait_ge(flag_turned, 1)
            nc.vector.tensor_copy(use_counts[:, :], psA[:, 2, 0:1]).then_inc(flag_ready, 1)
            dve.wait_ge(src_ready, 2)
            link(nc.vector.tensor_scalar(src_hi, src_all[:, 0:COUNTED, :], P.bit_length() - 1, None, ALU.arith_shift_right))
            link(nc.vector.tensor_scalar(src_lo, src_all[:, 0:BUILDS, :], P - 1, None, ALU.bitwise_and))
            link(nc.vector.memset(cell_all[:, COUNTED:BUILDS, :], -1.0))
            link(nc.vector.scalar_tensor_tensor(out=cell_all[:, 0:COUNTED, :], in0=src_hi, scalar=float(CW),
                                                in1=loc_all[:, 0:COUNTED, :], op0=ALU.mult, op1=ALU.add))
            link(nc.vector.tensor_copy(src_lo_all[:, :, :], src_lo))

            def norm_rows(q, version):
                for g in range(GROUPS):
                    if q == 0:
                        if g == 0:
                            dve.wait_ge(pad_cleared, 1)
                        dve.wait_ge(x_loaded[g], 16)
                    for b in group_blocks(g):
                        last = nc.vector.bn_stats(ln_stats[:, b, :], rows_x[:, b, :])
                link(last)
                for b in range(BLOCKS):
                    last = nc.vector.bn_aggr(ln_mv[:, b, :], ln_stats[:, b, :])
                last.then_inc(ln_var_ready, 1)
                dve.wait_ge(ln_std_ready, q + 1)
                link(nc.vector.reciprocal(ln_rstd[:, :], ln_rstd[:, :]))
                if version > 0:
                    dve.wait_ge(table_written, 16 * LG * version)
                for g in range(GROUPS):
                    for b in group_blocks(g):
                        last = nc.vector.tensor_scalar(rows_h[:, b, :], rows_x[:, b, :], ln_mv[:, b, 0:1],
                                                       ln_rstd[:, b:b + 1], ALU.subtract, ALU.mult)
                    last.then_inc(normed, 1)

            def window_add(window, first, width):
                cols = acc[:, bass.DynSlice(first, width)]
                return nc.vector.tensor_tensor(cols, cols, window, ALU.add)

            def edges(layer):
                before = turns_before(layer, left)
                with dve.Fori(0, turns_of(layer, left)) as k:
                    n = dve.snap(k + before + 1)
                    super0 = dve.snap(k * SLOTS + (0 if layer < 2 else skipped * SLOTS)).with_bounds(min_val=0, max_val=SUPERS - SLOTS)
                    if layer < 2:
                        build = dve.snap(k + layer * TURNS)
                        dve.wait_ge(counted, n)
                        for j in range(EPP):
                            nc.vector.tensor_scalar(
                                cells[:, j, :], iota_c[:, :],
                                cell_all[:, bass.DynSlice(build, 1), j:j + 1].rearrange("p o j -> p (o j)"), None,
                                ALU.is_equal)
                        nc.vector.tensor_tensor(
                            src_hot[:, :, :], iota0[:, :].unsqueeze(1).broadcast_to((P, EPP, P)),
                            src_lo_all[:, bass.DynSlice(build, 1), :].rearrange("p o j -> p (o j)").unsqueeze(2
                            ).broadcast_to((P, EPP, P)), ALU.is_equal).then_inc(cells_ready, 1)
                        n16 = dve.snap(n * 16)
                        for u in range(SLOTS):
                            for j in range(EPP):
                                dve.wait_ge(gathered[u][j], n16)
                            dve.wait_ge(ea_loaded[u], n16)
                            nc.vector.tensor_tensor(ea[:, u, :, :], ea[:, u, :, :], xg[:, u, :, :],
                                                    ALU.add).then_inc(summed[u], 1)
                    with dve.Fori(0, rounds) as r:
                        v = dve.snap((k + before) * rounds + r + 1)
                        nxt = dve.snap(v + 1)
                        nc.vector.tensor_scalar(first_i[:, :], base_f[:, bass.DynSlice(super0, SLOTS)],
                                                round_off[0:1, bass.DynSlice(r, 1)], float(NODES),
                                                ALU.add, ALU.min).then_inc(firsts_ready, 1)

                        def add_window(u):
                            first = dve.value_load(first_i[0:1, u:u + 1], min_val=0, max_val=NODES)
                            dve.wait_ge(reduced[u], nxt)
                            dve.wait_ge(added[(u - 1) % SLOTS], nxt if u else v)
                            if layer >= 2 and u == 0:
                                dve.wait_ge(counts_added, counts_before)
                            window_add(psG[:, u, 0:WIN], first, WIN).then_inc(added[u], 1)

                        if layer >= 2:
                            counts_before = dve.snap((k + (layer - 2) * left) * SLOTS + 1)
                        for u in range(SLOTS):
                            if u == 0:
                                dve.wait_ge(firsts_ready, v)
                            dve.wait_ge(reduced[u], v)
                            loc = loc_all[:, bass.DynSlice(super0 + u, 1), :].rearrange("p o j -> p (o j)")
                            nc.vector.scalar_tensor_tensor(
                                out=hot[:, u, :, :], in0=loc.unsqueeze(2).broadcast_to((P, EPP, WIN)),
                                scalar=round_off[:, bass.DynSlice(r, 1)],
                                in1=iota0[:, :].unsqueeze(1).broadcast_to((P, EPP, WIN)),
                                op0=ALU.subtract, op1=ALU.is_equal).then_inc(hot_ready[u], 1)
                            if u > 0:
                                add_window(u - 1)
                        add_window(SLOTS - 1)
                    if layer >= 2:
                        m = dve.snap(k + (layer - 2) * left + 2)
                        group = dve.snap(k * use).with_bounds(min_val=0, max_val=TURNS - SKIP - 1)
                        for w in range(SLOTS):
                            first = dve.value_load(base_i[0:1, bass.DynSlice(group * SLOTS + w, 1)],
                                                   min_val=0, max_val=NODES)
                            if w == 0:
                                dve.wait_ge(products_out, m)
                                dve.wait_ge(added[SLOTS - 1], dve.snap((k + before + 1) * rounds + 1))
                            else:
                                dve.wait_ge(counts_added, dve.snap((k + (layer - 2) * left) * SLOTS + (w + 1)))
                            window_add(product[:, w, :], first, CW).then_inc(counts_added, 1)

            def split_features(layer):
                for c, (a, b) in enumerate(SPLIT):
                    dve.wait_ge(hi_ready, (layer - 2) * NSPLIT + c + 1)
                    nc.vector.scalar_tensor_tensor(out=hid_rows[:, a:b, :], in0=rows_h[:, a:b, :], scalar=use_counts[:, 0:1],
                                                   in1=xp[:, a:b, 0, :], op0=ALU.mult, op1=ALU.subtract).then_inc(rest_ready, 1)
                for c, (a, b) in enumerate(SPLIT):
                    dve.wait_ge(mid_ready, (layer - 2) * NSPLIT + c + 1)
                    nc.vector.tensor_tensor(xp[:, a:b, 2, :], hid_rows[:, a:b, :], xp[:, a:b, 1, :],
                                            ALU.subtract).then_inc(parts_ready, 1)

            def mlp(layer):
                if layer < 2:
                    for g in range(GROUPS):
                        c0, _ = group_cols(g)
                        dve.wait_ge(hid_ready, layer * LG + g + 1)
                        last = nc.vector.bn_stats(bn_stats[:, g, :], hid[:, c0:c0 + real_cols(g)])
                    last.then_inc(bn_step, 1)
                    dve.wait_ge(bn_step, 4 * layer + 1)
                    nc.vector.bn_aggr(bn_mv[:, :], bn_stats[:, :, :].rearrange("p g k -> p (g k)")).then_inc(bn_var_ready, 1)
                    dve.wait_ge(bn_std_ready, layer + 1)
                    nc.vector.reciprocal(bn_tmp[:, :], bn_std[:, :]).then_inc(bn_step, 1)
                    dve.wait_ge(bn_step, 4 * layer + 2)
                    nc.vector.tensor_tensor(bn_scale[:, :], bn_tmp[:, :], bn_gamma[:, layer:layer + 1], ALU.mult).then_inc(bn_step, 1)
                    dve.wait_ge(bn_step, 4 * layer + 3)
                    nc.vector.tensor_tensor(bn_tmp[:, :], bn_mv[:, 0:1], bn_scale[:, :], ALU.mult).then_inc(bn_step, 1)
                    dve.wait_ge(bn_step, 4 * layer + 4)
                    nc.vector.tensor_tensor(bn_shift[:, :], bn_beta[:, layer:layer + 1], bn_tmp[:, :], ALU.subtract).then_inc(bn_ready, 1)
                for g in range(GROUPS):
                    c0, w = group_cols(g)
                    dve.wait_ge(second_done, layer * LG + g + 1)
                    b = bias_second[:, layer:layer + 1]
                    if layer < 3:
                        ins = nc.vector.tensor_scalar(acc[:, c0:c0 + w], psA[:, g % 4, 0:w], b, 0.0, ALU.add, ALU.max)
                    else:
                        ins = nc.vector.tensor_scalar(acc[:, c0:c0 + w], psA[:, g % 4, 0:w], b, None, ALU.add)
                    ins.then_inc(next_ready, 1)
                if layer == 1:
                    for g in range(GROUPS):
                        b0, nb = g * GB, len(group_blocks(g))
                        dve.wait_ge(rows_turned, layer * LG + g + 1)
                        nc.vector.tensor_tensor(rows_x[:, b0:b0 + nb, :], rows_x[:, b0:b0 + nb, :],
                                                psG[:, g % 4, 0:nb * P].rearrange("p (b d) -> p b d", d=D), ALU.add
                                                ).then_inc(resid_ready, 1)
                    dve.wait_ge(resid_ready, GROUPS)
                if layer == 2:
                    for g in range(GROUPS):
                        c0, w = group_cols(g)
                        dve.wait_ge(rows_turned, layer * LG + g + 1)
                        nc.vector.tensor_scalar(acc[:, c0:c0 + w], acc[:, c0:c0 + w], one_eps[:, 1:2], None,
                                                ALU.mult).then_inc(acc_scaled, 1)
                if layer == 3:
                    dve.wait_ge(table_written, 16 * LG * LAYERS)
                    for g in range(GROUPS):
                        b0, nb = g * GB, len(group_blocks(g))
                        dve.wait_ge(rows_turned, layer * LG + g + 1)
                        nc.vector.tensor_tensor(rows_h[:, b0:b0 + nb, :], rows_x[:, b0:b0 + nb, :],
                                                psG[:, g % 4, 0:nb * P].rearrange("p (b d) -> p b d", d=D), ALU.add
                                                ).then_inc(rows_ready, 1)

            norm_rows(0, 0)
            dve.wait_ge(params_loaded, PARAMS)
            for k in range(2):
                nc.vector.tensor_scalar(one_eps[:, k:k + 1], eps_col[:, k:k + 1], 1.0, None, ALU.add).then_inc(weights_ready, 1)
            rounds, skipped, left, use = load_plan(dve)
            dve.wait_ge(more_consts, 3)
            for layer in range(LAYERS):
                if layer in (0, 2):
                    dve.wait_ge(cols_ready, (layer // 2 + 1) * LG)
                    dve.wait_ge(consts_made, 5)
                elif layer == 1:
                    dve.wait_ge(next_ready, 1 * LG)
                else:
                    dve.wait_ge(acc_scaled, LG)
                if layer >= 2:
                    split_features(layer)
                edges(layer)
                mlp(layer)
                if layer == 1:
                    norm_rows(1, 2)

        @block.tensor
        def _(pe):
            for u in range(SLOTS):
                pe.sem_inc(reduced[u], 1)
            pe.sem_inc(counted, 1)
            for h in range(2):
                pe.sem_inc(counts_used[h], 1)
            pe.wait_ge(consts_made, 5)

            def turn_indices(tables, ready, bank0, done):
                for h, rows in ((0, FIRST), (1, SECOND)):
                    pe.wait_ge(ready, h + 1)
                    for j in range(EPP):
                        last = nc.tensor.transpose(psG[:, bank0 + h, j * P:j * P + rows],
                                                   flt[0:rows, tables + h, j::EPP], ident[0:rows, 0:rows])
                    last.then_inc(done, 1)

            turn_indices(0, src_float, 0, src_turned)
            turn_indices(2, loc_float, 2, loc_turned)
            pe.wait_ge(stat_ready, 2)
            for h, rows in ((0, FIRST), (1, SECOND)):
                for k, col in ((0, 0), (1, 2)):
                    last = nc.tensor.matmul(psA[0:1, k, h * FIRST:h * FIRST + rows], win_stat[0:rows, h, col:col + 1],
                                            ident[0:rows, 0:rows], start=(h == 0), stop=True, skip_group_check=True)
            last.then_inc(base_turned, 1)
            pe.wait_ge(flag_ready, 1)
            pe.wait_ge(more_consts, 3)
            nc.tensor.matmul(psA[:, 2, 0:1], ones_row[0:1, :], plan_f[0:1, 3:4], start=True, stop=True).then_inc(flag_turned, 1)
            pe.wait_ge(loc_ready, 2)
            pe.wait_ge(src_ready, 2)

            def turn_rows(q):
                for g in range(GROUPS):
                    pe.wait_ge(rows_ready, (0, 2)[q] * LG + g + 1)
                    if g >= 4:
                        pe.wait_ge(cols_ready, q * LG + g - 3)
                    for k, b in enumerate(group_blocks(g)):
                        last = nc.tensor.transpose(psG[:, g % 4, k * P:(k + 1) * P], rows_h[:, b, :], ident[:, :])
                    last.then_inc(cols_turned, 1)

            def build_counts(n):
                pe.wait_ge(cells_ready, n)
                pe.wait_ge(count_evicted, n)
                for j in range(EPP):
                    for bank, c0 in enumerate(range(0, CB, CBANK * CW)):
                        w = min(CBANK * CW, CB - c0)
                        last = nc.tensor.matmul(psA[:, bank, 0:w], src_hot[:, j, :], cells[:, j, c0:c0 + w],
                                                start=(j == 0), stop=(j == EPP - 1))
                last.then_inc(counted, 1)

            def multiply_counts(layer, k):
                pe.wait_ge(products_out, pe.snap(k + (layer - 2) * left + 1))
                n16 = pe.snap((k + (layer - 2) * left + 1) * 16)
                out_cols = psA[:, 0, 0:SLOTS * CW].rearrange("p (s c) -> p s c", s=SLOTS)
                for h, (b0, b1_) in enumerate(((0, HALF_B), (HALF_B, BLOCKS))):
                    pe.wait_ge(counts_loaded[h], n16)
                    for b in range(b0, b1_):
                        for part in range(PARTS):
                            last = nc.tensor.matmul(out_cols, xp[:, b, part, :], counts[:, :, b * CW:(b + 1) * CW],
                                                    start=(b == 0 and part == 0),
                                                    stop=(b == BLOCKS - 1 and part == PARTS - 1))
                    last.then_inc(counts_used[h], 1)

            def edges(layer):
                before = turns_before(layer, left)
                if layer >= 2:
                    pe.wait_ge(parts_ready, (layer - 1) * NSPLIT)
                with pe.Fori(0, turns_of(layer, left)) as k:
                    n = pe.snap(k + before + 1)
                    if layer < 2:
                        build_counts(n)
                    else:
                        multiply_counts(layer, k)
                        n16 = pe.snap(n * 16)
                    with pe.Fori(0, rounds) as r:
                        v = pe.snap((k + before) * rounds + r + 1)
                        for u in range(SLOTS):
                            pe.wait_ge(added[u], v)
                            pe.wait_ge(hot_ready[u], v)
                            if layer < 2:
                                pe.wait_ge(msg_ready[u], n)
                            for j in range(EPP):
                                if layer >= 2:
                                    pe.wait_ge(gathered[u][j], n16)
                                msg = ea if layer < 2 else xg
                                last = nc.tensor.matmul(psG[:, u, 0:WIN], msg[:, u, j, :], hot[:, u, j, :],
                                                        start=(j == 0), stop=(j == EPP - 1))
                            last.then_inc(reduced[u], 1)

            def mlp(layer):
                for u in range(SLOTS):
                    pe.wait_ge(added[u], pe.snap(rounds * turns_before(layer + 1, left) + 1))
                if layer < 2:
                    pe.wait_ge(count_evicted, (layer + 1) * TURNS + 1)
                else:
                    pe.wait_ge(counts_added, pe.snap(left * (SLOTS * (layer - 1)) + 1))
                for g in range(GROUPS):
                    c0, w = group_cols(g)
                    if g >= 4:
                        pe.wait_ge(hid_ready, layer * LG + g - 3)
                    nc.tensor.matmul(psG[:, g % 4, 0:w], w_first[:, layer, :], acc[:, c0:c0 + w],
                                     start=True, stop=True).then_inc(first_done, 1)
                for g in range(GROUPS):
                    c0, w = group_cols(g)
                    pe.wait_ge(act_ready if layer < 2 else hid_ready, layer * LG + g + 1)
                    if g >= 4:
                        pe.wait_ge(next_ready, layer * LG + g - 3)
                    nc.tensor.matmul(psA[:, g % 4, 0:w], w_second[:, layer, :], hid[:, c0:c0 + w],
                                     start=True, stop=True).then_inc(second_done, 1)
                for g in range(GROUPS):
                    pe.wait_ge(next_ready, layer * LG + g + 1)
                    if g >= 4:
                        pe.wait_ge({0: rows_ready, 1: resid_ready, 2: rows_ready, 3: rows_ready}[layer],
                                   {0: 1, 1: 0, 2: 3, 3: 4}[layer] * LG + g - 3)
                    elif layer >= 2:
                        pe.wait_ge(hid_ready, (layer + 1) * LG)
                    for k, b in enumerate(group_blocks(g)):
                        last = nc.tensor.transpose(psG[:, g % 4, k * P:(k + 1) * P], acc[:, b * P:(b + 1) * P], ident[:, :])
                    last.then_inc(rows_turned, 1)

            turn_rows(0)
            pe.wait_ge(params_loaded, PARAMS)
            pe.wait_ge(cols_ready, LG)
            for k in range(4):
                last = nc.tensor.transpose(psG[:, 1, k * P:(k + 1) * P], w_rows[:, k, :], ident[:, :])
            last.then_inc(weights_turned, 1)
            pe.wait_ge(weights_ready, 6)
            pe.wait_ge(flag_ready, 2)
            rounds, skipped, left, use = load_plan(pe)
            for layer in range(LAYERS):
                edges(layer)
                mlp(layer)
                if layer == 1:
                    turn_rows(1)


_INS = ['x', 'src', 'dst', 'edge_attr_128', 'L0_gnn_W1', 'L0_gnn_b1', 'L0_gnn_gamma', 'L0_gnn_beta', 'L0_gnn_W2',
        'L0_gnn_b2', 'L1_gnn_w1a', 'L1_gnn_b1a', 'L1_gnn_w1b', 'L1_gnn_b1b', 'L1_gnn_eps1', 'L1_gnn_w2a',
        'L1_gnn_b2a', 'L1_gnn_w2b', 'L1_gnn_b2b', 'L1_gnn_eps2']


def kernel(**inputs):
    import numpy as _np
    import concourse.bacc as _bacc
    from concourse import mybir as _mybir
    from concourse.bass_utils import run_bass_kernel_spmd as _run

    nc = _bacc.Bacc("TRN2", target_bir_lowering=False, num_devices=1)
    arrays, args = {}, []
    for name in _INS:
        a = _np.ascontiguousarray(_np.atleast_1d(_np.asarray(inputs[name])))
        arrays[f"in_{name}_dram"] = a
        args.append(nc.dram_tensor(f"in_{name}_dram", a.shape, _mybir.dt.from_np(a.dtype), kind="ExternalInput").ap())
    out = nc.dram_tensor("out_dram", (NODES, D), F32, kind="ExternalOutput").ap()
    gnn_kernel(nc, *args, out)
    r = _run(nc, [arrays], core_ids=[0])
    return r.results[0]["out_dram"]
```

```python
from contextlib import ExitStack

import concourse.bass as bass
from concourse import mybir

ALU = mybir.AluOpType
ACT = mybir.ActivationFunctionType
AX_X = mybir.AxisListType.X
F32 = mybir.dt.float32
I32 = mybir.dt.int32
I16 = mybir.dt.int16
F16 = mybir.dt.float16
BF16 = mybir.dt.bfloat16

P = 128
NODES = 6250
EDGES = 100000
D = 128
EPP = 4
SUP = P * EPP
SUPERS = -(-EDGES // SUP)
TAIL_START = EDGES - SUP
OVERLAP = SUPERS * SUP - EDGES
SLOTS = 4
TURNS = SUPERS // SLOTS
WIN = 128
BLOCKS = -(-NODES // P)
PADDED = BLOCKS * P
ACC = PADDED + WIN
GB = 4
GROUPS = -(-BLOCKS // GB)
FIRST = P
SECOND = SUPERS - FIRST
LAST_BLOCK = NODES - (BLOCKS - 1) * P
CW = 41
CB = BLOCKS * CW
CBANKS = -(-CB // 512)
UNITS = 2 * TURNS
PAIRS = 18
COUNTED = UNITS + PAIRS
SKIP = COUNTED // SLOTS
UPT = -(-UNITS // (TURNS - SKIP))
KEPT = (TURNS - SKIP) * UPT
SPLIT = [(0, 12), (12, 24), (24, 36), (36, BLOCKS)]
HALF_B = SPLIT[1][1]
PARTS = 3
LN_EPS = 1e-5
BN_EPS = 1e-5
LAYERS = 4

assert SUPERS % SLOTS == 0 and OVERLAP % EPP == 0 and SECOND <= P
assert COUNTED == SKIP * SLOTS and COUNTED <= FIRST and CBANKS == 4 and UPT * CW <= 512


def group_blocks(g):
    return range(g * GB, min((g + 1) * GB, BLOCKS))


def group_cols(g):
    return g * GB * P, len(group_blocks(g)) * P


def real_cols(g):
    c0, n = group_cols(g)
    return min(n, NODES - c0)



def gnn_kernel(nc, x, src, dst, edge_attr, W1, b1, gamma, beta, W2, b2,
               w1a, b1a, w1b, b1b, eps1, w2a, b2a, w2b, b2b, eps2, out):
    with ExitStack() as ctx:
        ctx.enter_context(nc.allow_non_contiguous_dma(reason="columns of biases"))

        def sb(name, shape, dt=F32):
            return ctx.enter_context(nc.sbuf_tensor(name, shape, dt))

        def sem(name):
            return ctx.enter_context(nc.semaphore(name))

        count_store = nc.dram_tensor("count_store", [KEPT, P, CB], F16, kind="Internal").ap()
        table = nc.dram_tensor("node_table", [PADDED, D], F32, kind="Internal").ap()

        ident = sb("ident", [P, P])
        iota0 = sb("iota0", [P, WIN])
        iota_c = sb("iota_c", [P, CB], I16)
        round_off = sb("round_off", [P, BLOCKS])
        ones_row = sb("ones_row", [1, P])
        w_first = sb("w_first", [P, LAYERS, D])
        w_second = sb("w_second", [P, LAYERS, D])
        bias_first = sb("bias_first", [P, LAYERS])
        bias_second = sb("bias_second", [P, LAYERS])
        bn_gamma = sb("bn_gamma", [P, 2])
        bn_beta = sb("bn_beta", [P, 2])
        bias_last = sb("bias_last", [P, D])
        eps_col = sb("eps_col", [P, 2])
        one_eps = sb("one_eps", [P, 2])
        small_eps = sb("small_eps", [P, 1])
        hid = sb("hid", [P, PADDED])
        raw = hid[:, 0:4 * SUP].bitcast(I32).rearrange("p (t e) -> p t e", t=4)
        flt = hid[:, 4 * SUP:8 * SUP].rearrange("p (t e) -> p t e", t=4)
        src_hi = hid[:, 8 * SUP:8 * SUP + COUNTED * EPP].bitcast(I32).rearrange("p (s j) -> p s j", j=EPP)
        src_lo = hid[:, 9 * SUP:9 * SUP + COUNTED * EPP].bitcast(I32).rearrange("p (s j) -> p s j", j=EPP)
        win_stat = sb("win_stat", [P, 2, 3])
        src_all = sb("src_all", [P, SUPERS + SLOTS, EPP], I32)
        loc_all = sb("loc_all", [P, SUPERS, EPP])
        base_f = sb("base_f", [1, SUPERS])
        spare = hid[0:1, 10 * SUP:12 * SUP]
        unit_f = spare[:, 0:3 * KEPT].rearrange("o (k s) -> o k s", k=3)
        unit_i = sb("unit_i", [1, KEPT], I32)
        shift_f = spare[:, SUP:SUP + 2 * PAIRS]
        last_f = spare[:, 3 * SUP // 2:3 * SUP // 2 + COUNTED]
        plan_f = sb("plan_f", [1, 4])
        rounds_wide = sb("rounds_wide", [1, 1], I32)
        plan_i = sb("plan_i", [1, 4], I32)
        use_counts = sb("use_counts", [P, 1])
        cell_all = sb("cell_all", [P, COUNTED, EPP])
        src_lo_all = sb("src_lo_all", [P, COUNTED, EPP])
        rows_x = sb("rows_x", [P, BLOCKS, D])
        rows_h = sb("rows_h", [P, BLOCKS, D])
        acc = sb("acc", [P, ACC])
        hid_rows = hid[:, :].rearrange("p (b d) -> p b d", d=D)
        ln_tmp = sb("ln_tmp", [P, 3, BLOCKS])
        ln_neg_mean = sb("ln_neg_mean", [P, BLOCKS])
        ln_var = sb("ln_var", [P, BLOCKS])
        ln_rstd = sb("ln_rstd", [P, BLOCKS])
        bn_stats = sb("bn_stats", [P, GROUPS, 6])
        bn_mv = sb("bn_mv", [P, 2])
        bn_std = sb("bn_std", [P, 1])
        bn_scale = sb("bn_scale", [P, 1])
        bn_shift = sb("bn_shift", [P, 1])
        bn_tmp = sb("bn_tmp", [P, 1])
        idx = sb("idx", [P, SLOTS, EPP], I32)
        xg = sb("xg", [P, SLOTS, EPP, D])
        ea = sb("ea", [P, SLOTS, EPP, D])
        hot = sb("hot", [P, SLOTS, EPP, WIN])
        first_i = sb("first_i", [1, SLOTS], I32)
        cells = sb("cells", [P, UPT, CB], F16)
        counts = cells
        product = sb("product", [P, UPT, CW])
        count_out = sb("count_out", [P, CB], F16)
        xp_room = sb("xp_room", [P, BLOCKS * PARTS * D], BF16)
        xp = xp_room[:, :].rearrange("p (b q d) -> p b q d", q=PARTS, d=D)
        w_rows = xp_room[:, 0:8 * D].bitcast(F32).rearrange("p (k d) -> p k d", d=D)
        src_hot = xp_room[:, 8 * D:(8 + EPP) * D].bitcast(F16).rearrange("p (j d) -> p j d", d=D)
        ln_stats = xp_room[:, (8 + EPP) * D:(8 + EPP) * D + 12 * BLOCKS].bitcast(F32).rearrange("p (b k) -> p b k", k=6)

        psG = ctx.enter_context(nc.psum_tensor("psG", [P, 4, 512], F32))
        psA = ctx.enter_context(nc.psum_tensor("psA", [P, 4, 512], F32))

        params_loaded = sem("params_loaded")
        x_loaded = [sem(f"x_loaded{g}") for g in range(GROUPS)]
        src_loaded = sem("src_loaded")
        dst_loaded = sem("dst_loaded")
        consts_made = sem("consts_made")
        pad_cleared = sem("pad_cleared")
        weights_turned = sem("weights_turned")
        weights_ready = sem("weights_ready")
        src_float = sem("src_float")
        src_turned = sem("src_turned")
        src_ready = sem("src_ready")
        loc_float = sem("loc_float")
        loc_turned = sem("loc_turned")
        loc_ready = sem("loc_ready")
        stat_ready = sem("stat_ready")
        base_turned = sem("base_turned")
        unit_step = sem("unit_step")
        shift_ready = sem("shift_ready")
        flag_turned = sem("flag_turned")
        flag_ready = sem("flag_ready")
        zeros_made = sem("zeros_made")
        more_consts = sem("more_consts")
        plan_ready = sem("plan_ready")
        vec = sem("vec")
        ln_var_ready = sem("ln_var_ready")
        ln_std_ready = sem("ln_std_ready")
        centred = sem("centred")
        bias_added = sem("bias_added")
        rows_ready = sem("rows_ready")
        table_written = sem("table_written")
        cols_turned = sem("cols_turned")
        cols_ready = sem("cols_ready")
        first_done = sem("first_done")
        hid_ready = sem("hid_ready")
        bn_var_ready = sem("bn_var_ready")
        bn_std_ready = sem("bn_std_ready")
        bn_ready = sem("bn_ready")
        act_ready = sem("act_ready")
        second_done = sem("second_done")
        next_ready = sem("next_ready")
        rows_turned = sem("rows_turned")
        acc_scaled = sem("acc_scaled")
        resid_ready = sem("resid_ready")
        hi_ready = sem("hi_ready")
        rest_ready = sem("rest_ready")
        mid_ready = sem("mid_ready")
        parts_ready = sem("parts_ready")
        firsts_ready = [sem(f"firsts_ready{g}") for g in range(2)]
        slots_opened = sem("slots_opened")
        bn_step = sem("bn_step")
        out_written = sem("out_written")

        idx_ready = [sem(f"idx_ready{u}") for u in range(SLOTS)]
        gathered = [[sem(f"gathered{u}_{j}") for j in range(EPP)] for u in range(SLOTS)]
        ea_loaded = [sem(f"ea_loaded{u}") for u in range(SLOTS)]
        cells_ready = sem("cells_ready")
        count_stored = sem("count_stored")
        counts_loaded = [sem(f"counts_loaded{h}") for h in range(2)]
        summed = [sem(f"summed{u}") for u in range(SLOTS)]
        reduced = [sem(f"reduced{u}") for u in range(SLOTS)]
        added = [sem(f"added{u}") for u in range(SLOTS)]
        cells_used = sem("cells_used")
        counted = sem("counted")
        count_evicted = sem("count_evicted")
        counts_used = [sem(f"counts_used{h}") for h in range(2)]
        products_out = sem("products_out")
        counts_added = sem("counts_added")
        msg_ready = [sem(f"msg_ready{u}") for u in range(SLOTS)]
        hot_ready = [sem(f"hot_ready{u}") for u in range(SLOTS)]

        table_b = table.rearrange("(b p) d -> p b d", p=P)
        LG = GROUPS
        PARAMS = 16 * (2 * 6 + 4 + 3 + 1 + 2)

        CENTRED = (GROUPS - 4, GROUPS)
        LAG = 2

        NSPLIT = len(SPLIT)

        def load_plan(eng):
            eng.wait_ge(plan_ready, 3)
            return (eng.value_load(plan_i[0:1, 0:1], min_val=1, max_val=BLOCKS),
                    eng.value_load(plan_i[0:1, 1:2], min_val=0, max_val=SKIP),
                    eng.value_load(plan_i[0:1, 2:3], min_val=TURNS - SKIP, max_val=TURNS),
                    eng.value_load(plan_i[0:1, 3:4], min_val=0, max_val=1))

        def turns_before(layer, left):
            return layer * TURNS if layer < 2 else 2 * TURNS + (layer - 2) * left

        BUILD_TURNS = ([(0, PAIRS, 2), (PAIRS, TURNS, 1)], [(0, TURNS, 1)])

        def first_counted(layer, supers, k):
            return k * 2 if supers == 2 else k + (layer * TURNS + PAIRS)

        WINDOW_SLOTS = ([range(SLOTS)], [range(SLOTS)], [range(0, 2), range(2, SLOTS)], [range(0, 2), range(2, SLOTS)])

        def turns_of(layer, left):
            return TURNS if layer < 2 else left

        block = ctx.enter_context(nc.Block())

        @block.sync
        def _(sp):
            def load_indices(arr, k, loaded):
                half = FIRST * SUP
                sp.dma_start(raw[:, k, :], arr[0:half].rearrange("(s e) -> s e", e=SUP)).then_inc(loaded, 16)
                sp.dma_start(raw[0:SECOND - 1, k + 1, :],
                             arr[half:half + (SECOND - 1) * SUP].rearrange("(s e) -> s e", e=SUP)).then_inc(loaded, 16)
                sp.dma_start(raw[SECOND - 1:SECOND, k + 1, :],
                             arr[TAIL_START:EDGES].rearrange("(s e) -> s e", s=1)).then_inc(loaded, 16)

            load_indices(src, 0, src_loaded)
            sp.wait_ge(pad_cleared, 1)
            for g in range(GROUPS):
                b0, nb = g * GB, len(group_blocks(g))
                if g < GROUPS - 1:
                    sp.dma_start(rows_x[:, b0:b0 + nb, :],
                                 x[b0 * P:(b0 + nb) * P, :].rearrange("(b p) d -> p b d", p=P)).then_inc(x_loaded[g], 16)
                else:
                    sp.dma_start(rows_x[0:LAST_BLOCK, b0, :], x[b0 * P:NODES, :]).then_inc(x_loaded[g], 16)
            load_indices(dst, 2, dst_loaded)
            for l in range(2):
                sp.dma_start(w_first[:, l, :], W1[l]).then_inc(params_loaded, 16)
                sp.dma_start(w_second[:, l, :], W2[l]).then_inc(params_loaded, 16)
                for dst_col, a in ((bias_first[:, l:l + 1], b1), (bias_second[:, l:l + 1], b2),
                                   (bn_gamma[:, l:l + 1], gamma), (bn_beta[:, l:l + 1], beta)):
                    sp.dma_start(dst_col, a[l:l + 1, :].rearrange("o d -> d o")).then_inc(params_loaded, 16)
            for k, a in enumerate((w1a, w1b, w2a, w2b)):
                sp.dma_start(w_rows[:, k, :], a).then_inc(params_loaded, 16)
            for dst_col, a in ((bias_first[:, 2:3], b1a), (bias_second[:, 2:3], b1b), (bias_first[:, 3:4], b2a)):
                sp.dma_start(dst_col, a.rearrange("(d o) -> d o", o=1)).then_inc(params_loaded, 16)
            sp.dma_start(bias_last[:, :], b2b.rearrange("(o d) -> o d", o=1).broadcast_to((P, D))).then_inc(params_loaded, 16)
            for k, a in enumerate((eps1, eps2)):
                sp.dma_start(eps_col[:, k:k + 1],
                             a.rearrange("(o e) -> o e", o=1).broadcast_to((P, 1))).then_inc(params_loaded, 16)

            def load_supertile(u, first):
                sp.dma_start(ea[:, u, :, :].rearrange("p j d -> p (j d)"),
                             edge_attr[bass.DynSlice(first, SUP), :].rearrange("(p j) d -> p (j d)", j=EPP)
                             ).then_inc(ea_loaded[u], 16)

            def store_table(version):
                for g in range(GROUPS):
                    b0, nb = g * GB, len(group_blocks(g))
                    sp.wait_ge(rows_ready, version * LG + g + 1)
                    sp.dma_start(table_b[:, b0:b0 + nb, :], rows_h[:, b0:b0 + nb, :]).then_inc(table_written, 16)

            def store_counts(n, built):
                sp.wait_ge(count_evicted, built + 1)
                sp.dma_start(count_store[bass.DynSlice(n, 1)].rearrange("o p c -> (o p) c"),
                             count_out[:, :]).then_inc(count_stored, 16)

            def load_edges(layer):
                turn0 = layer * TURNS
                if layer > 0:
                    for u in range(SLOTS):
                        sp.wait_ge(reduced[u], sp.snap(rounds * turn0 + 1))
                        load_supertile(u, u * SUP)
                with sp.Fori(1, TURNS - 1) as k:
                    last_use = sp.snap((k + turn0) * rounds + 1)
                    for u in range(SLOTS):
                        sp.wait_ge(reduced[u], last_use)
                        load_supertile(u, (k * SLOTS + u) * SUP)
                    store_counts(k + (turn0 - 1), sp.snap(k + turn0))
                last_use = sp.snap(rounds * (turn0 + TURNS - 1) + 1)
                for u in range(SLOTS):
                    sp.wait_ge(reduced[u], last_use)
                    load_supertile(u, min(((TURNS - 1) * SLOTS + u) * SUP, TAIL_START))
                for n in (turn0 + TURNS - 2, turn0 + TURNS - 1):
                    store_counts(n, n + 1)

            def load_counts(layer):
                with sp.Fori(0, left) as k:
                    group = sp.snap(k * use).with_bounds(min_val=0, max_val=TURNS - SKIP - 1)
                    n = sp.snap(k + (layer - 2) * left + 1)
                    for h, b in ((0, slice(0, HALF_B * CW)), (1, slice(HALF_B * CW, CB))):
                        sp.wait_ge(counts_used[h], n)
                        sp.dma_start(counts[:, :, b],
                                     count_store[bass.DynSlice(group * UPT, UPT), :, b].rearrange("s p c -> p s c")
                                     ).then_inc(counts_loaded[h], 16)

            for u in range(SLOTS):
                load_supertile(u, u * SUP)
            store_table(0)
            sp.wait_ge(zeros_made, 1)
            for a in range(UNITS, KEPT):
                sp.dma_start(count_store[a], count_out[:, :]).then_inc(count_stored, 16)
            rounds, skipped, left, use = load_plan(sp)
            load_edges(0)
            store_table(1)
            load_edges(1)
            store_table(2)
            sp.wait_ge(counted, 2 * TURNS + 1)
            sp.wait_ge(count_stored, 16 * KEPT)
            load_counts(2)
            store_table(3)
            load_counts(3)
            for g in range(GROUPS):
                b0, nb = g * GB, len(group_blocks(g))
                sp.wait_ge(rows_ready, LAYERS * LG + g + 1)
                if g < GROUPS - 1:
                    sp.dma_start(out[b0 * P:(b0 + nb) * P, :].rearrange("(b p) d -> p b d", p=P),
                                 rows_h[:, b0:b0 + nb, :]).then_inc(out_written, 16)
                else:
                    sp.dma_start(out[b0 * P:NODES, :], rows_h[0:LAST_BLOCK, b0, :]).then_inc(out_written, 16)
            sp.wait_ge(out_written, 16 * GROUPS)

        @block.gpsimd
        def _(pool):
            nc.gpsimd.memset(rows_x[:, BLOCKS - 1, :], 0.0).then_inc(pad_cleared, 1)
            nc.gpsimd.memset(acc[:, PADDED:ACC], 0.0).then_inc(consts_made, 1)
            nc.gpsimd.iota(iota0[:, :], pattern=[[1, WIN]], base=0, channel_multiplier=0,
                           allow_small_or_imprecise_dtypes=True).then_inc(consts_made, 1)
            nc.gpsimd.memset(small_eps[:, :], LN_EPS).then_inc(consts_made, 1)
            nc.gpsimd.memset(ident[:, :], 0.0).then_inc(consts_made, 1)
            pool.wait_ge(consts_made, 4)
            nc.gpsimd.affine_select(out=ident[:, :], in_=ident[:, :], compare_op=ALU.not_equal, fill=1.0,
                                    base=0, pattern=[[-1, P]], channel_multiplier=1).then_inc(consts_made, 1)
            nc.gpsimd.iota(iota_c[:, :], pattern=[[1, CB]], base=0, channel_multiplier=0).then_inc(more_consts, 1)
            nc.gpsimd.iota(round_off[:, :], pattern=[[WIN, BLOCKS]], base=0, channel_multiplier=0,
                           allow_small_or_imprecise_dtypes=True).then_inc(more_consts, 1)
            nc.gpsimd.memset(ones_row[:, :], 1.0).then_inc(more_consts, 1)
            nc.gpsimd.memset(count_out[:, :], 0.0).then_inc(zeros_made, 1)
            for layer in range(LAYERS):
                if layer == 2:
                    rounds, skipped, left, use = load_plan(pool)
                pool.wait_ge(table_written, 16 * GROUPS * (layer + 1))
                before = layer * TURNS if layer < 2 else turns_before(layer, left)
                with pool.Fori(0, TURNS if layer < 2 else left) as k:
                    n = pool.snap(k + before + 1)
                    freed = n if layer < 2 else pool.snap((k + before) * rounds + 1)
                    for u in range(SLOTS):
                        pool.wait_ge(idx_ready[u], n)
                        pool.wait_ge(summed[u] if layer < 2 else reduced[u], freed)
                        pool.sem_inc(slots_opened, 1)
                        for j in range(EPP):
                            nc.gpsimd.indirect_dma_start(
                                xg[:, u, j, :], None, table,
                                bass.IndirectOffsetOnAxis(ap=idx[:, u, j:j + 1], axis=0),
                            ).then_inc(gathered[u][j], 16)

        @block.scalar
        def _(act):
            act.sem_inc(count_evicted, 1)
            act.sem_inc(products_out, 1)
            for half in range(2):
                rows = (FIRST, SECOND)[half]
                act.wait_ge(src_turned, half + 1)
                act.copy(src_all[:, half * FIRST:half * FIRST + rows, :].rearrange("p s j -> p j s"),
                         psG[:, half, :].rearrange("p (j s) -> p j s", j=EPP)[:, :, 0:rows]).then_inc(src_ready, 1)
            act.wait_ge(src_ready, 2)
            act.copy(src_all[:, SUPERS:SUPERS + SLOTS, :], src_all[:, 0:SLOTS, :]).then_inc(src_ready, 1)
            for u in range(SLOTS):
                act.copy(idx[:, u, :], src_all[:, u, :]).then_inc(idx_ready[u], 1)
            def norm_rows(q, version):
                act.wait_ge(ln_var_ready, q + 1)
                act.activation(ln_rstd[:, :], ln_var[:, :], ACT.Sqrt, bias=small_eps[:, 0:1]).then_inc(ln_std_ready, 1)
                if version > 0:
                    act.wait_ge(table_written, 16 * LG * version)
                for g in range(CENTRED[q]):
                    for b in group_blocks(g):
                        last = act.activation(rows_h[:, b, :], rows_x[:, b, :], ACT.Relu, bias=ln_neg_mean[:, b:b + 1])
                    last.then_inc(centred, 1)

            def edges(layer):
                if layer == 1:
                    for u in range(SLOTS):
                        act.wait_ge(idx_ready[u], TURNS + 1)
                    act.copy(src_all[:, SUPERS:SUPERS + SLOTS, :],
                             src_all[:, bass.DynSlice((skipped * SLOTS), SLOTS), :]).then_inc(src_ready, 1)
                    act.wait_ge(src_ready, 4)
                with act.Fori(0, turns_of(layer, left)) as k:
                    before = turns_before(layer, left)
                    n = act.snap(k + before + 1)
                    if layer < 2:
                        nxt = act.snap(n + 1)
                    else:
                        n16 = act.snap(n * 16)
                        m = (layer - 2) * left + k + 1
                    first = 0 if layer < 2 else skipped * SLOTS
                    for u in range(SLOTS):
                        if layer >= 2 and u == 2:
                            act.wait_ge(counts_used[1], act.snap(m + 1))
                            act.wait_ge(counts_added, act.snap((m - 1) * UPT + 1))
                            act.copy(product[:, :, :], psA[:, 0, 0:UPT * CW].rearrange("p (s c) -> p s c", s=UPT)
                                     ).then_inc(products_out, 1)
                        if layer < 2:
                            act.wait_ge(summed[u], nxt)
                        else:
                            for j in range(EPP):
                                act.wait_ge(gathered[u][j], n16)
                        s = act.snap(k * SLOTS + (u + SLOTS) + first).with_bounds(min_val=0, max_val=SUPERS + SLOTS - 1)
                        act.copy(idx[:, u, :], src_all[:, bass.DynSlice(s, 1), :].rearrange("p o j -> p (o j)")
                                 ).then_inc(idx_ready[u], 1)
                        if layer < 2:
                            act.activation(ea[:, u, :, :], ea[:, u, :, :], ACT.Relu).then_inc(msg_ready[u], 1)
                    if layer < 2:
                        act.wait_ge(counted, nxt)
                        act.wait_ge(count_stored, act.snap(n * 16 + 16 * (KEPT - UNITS - 1)))
                        act.copy(count_out[:, :], psA[:, :, :].rearrange("p k c -> p (k c)")[:, 0:CB]).then_inc(count_evicted, 1)

            def split_features(layer):
                for c in range(NSPLIT + 1):
                    if c < NSPLIT:
                        a, b = SPLIT[c]
                        act.wait_ge(rows_ready, (layer + 1) * LG)
                        act.activation(xp[:, a:b, 0, :], rows_h[:, a:b, :], ACT.Copy,
                                       scale=use_counts[:, 0:1]).then_inc(hi_ready, 1)
                    if c > 0:
                        a, b = SPLIT[c - 1]
                        act.wait_ge(rest_ready, (layer - 2) * NSPLIT + c)
                        act.copy(xp[:, a:b, 1, :], hid_rows[:, a:b, :]).then_inc(mid_ready, 1)

            def hidden(layer, g):
                c0, w = group_cols(g)
                act.wait_ge(first_done, layer * LG + g + 1)
                bank = g % 4 if layer != 2 else g % 2
                act.activation(hid[:, c0:c0 + w], psG[:, bank, 0:w], ACT.Identity if layer < 2 else ACT.Relu,
                               bias=bias_first[:, layer:layer + 1]).then_inc(hid_ready, 1)

            def second_out(layer, g):
                c0, w = group_cols(g)
                act.wait_ge(second_done, layer * LG + g + 1)
                act.activation(acc[:, c0:c0 + w], psA[:, g % 4, 0:w], ACT.Relu,
                               bias=bias_second[:, layer:layer + 1]).then_inc(next_ready, 1)

            def rows_out(layer, g):
                b0, nb = g * GB, len(group_blocks(g))
                if g == 0:
                    act.wait_ge(table_written, 16 * LG * (1, None, 3)[layer])
                act.wait_ge(rows_turned, layer * LG + g + 1)
                bank = g % 4 if layer != 2 else 2 + g % 2
                act.copy(rows_h[:, b0:b0 + nb, :], psG[:, bank, 0:nb * P].rearrange("p (b d) -> p b d", d=D)
                         ).then_inc(rows_ready, 1)

            def mlp(layer):
                if layer < 2:
                    for g in range(GROUPS):
                        hidden(layer, g)
                    act.wait_ge(bn_var_ready, layer + 1)
                    act.activation(bn_std[:, :], bn_mv[:, 1:2], ACT.Sqrt, bias=small_eps[:, 0:1]).then_inc(bn_std_ready, 1)
                    act.wait_ge(bn_ready, layer + 1)
                    act.wait_ge(hid_ready, (layer + 1) * LG)
                behind = (LAG + 2, LAG - 1, 2 * LAG + 1, 0)[layer]
                for g in range(GROUPS + behind):
                    if g < GROUPS and layer < 2:
                        c0, w = group_cols(g)
                        act.activation(hid[:, c0:c0 + w], hid[:, c0:c0 + w], ACT.Relu, bias=bn_shift[:, 0:1],
                                       scale=bn_scale[:, 0:1]).then_inc(act_ready, 1)
                    elif g < GROUPS:
                        hidden(layer, g)
                    if g >= behind and layer != 3:
                        (second_out if layer == 1 else rows_out)(layer, g - behind)

            act.wait_ge(consts_made, 5)
            norm_rows(0, 0)
            for g in range(GROUPS):
                c0, w = group_cols(g)
                act.wait_ge(cols_turned, g + 1)
                act.copy(acc[:, c0:c0 + w], psG[:, g % 4, 0:w]).then_inc(cols_ready, 1)
            act.wait_ge(weights_turned, 1)
            for k in range(4):
                dst_w = (w_first, w_second)[k % 2]
                act.copy(dst_w[:, 2 + k // 2, :], psG[:, 1, k * P:(k + 1) * P]).then_inc(weights_ready, 1)
            rounds, skipped, left, use = load_plan(act)
            act.wait_ge(params_loaded, PARAMS)
            for layer in range(LAYERS):
                if layer >= 2:
                    split_features(layer)
                edges(layer)
                mlp(layer)
                if layer == 1:
                    norm_rows(1, 2)

        @block.vector
        def _(dve):
            steps = [0]

            def link(ins):
                steps[0] += 1
                ins.then_inc(vec, 1)
                dve.wait_ge(vec, steps[0])

            for u in range(SLOTS):
                dve.sem_inc(summed[u], 1)
                dve.sem_inc(added[u], 1)
            dve.sem_inc(counts_added, 1)

            halves = ((0, FIRST), (1, SECOND))
            dve.wait_ge(src_loaded, 48)
            for h, rows in halves:
                nc.vector.tensor_copy(flt[0:rows, h, :], raw[0:rows, h, :]).then_inc(src_float, 1)
            def stats_of(g):
                for b in group_blocks(g):
                    last = nc.vector.bn_stats(ln_stats[:, b, :], rows_x[:, b, :])
                return last

            def norm_rows(q):
                mean = lambda k: ln_stats[:, :, 3 * k + 1]
                sq = lambda k: ln_stats[:, :, 3 * k + 2]
                nc.vector.tensor_tensor(ln_tmp[:, 0, :], mean(0), mean(1), ALU.add)
                nc.vector.tensor_tensor(ln_tmp[:, 1, :], mean(0), mean(1), ALU.subtract)
                link(nc.vector.tensor_tensor(ln_tmp[:, 2, :], sq(0), sq(1), ALU.add))
                nc.vector.tensor_scalar(ln_neg_mean[:, :], ln_tmp[:, 0, :], -0.5, None, ALU.mult)
                link(nc.vector.scalar_tensor_tensor(out=ln_var[:, :], in0=ln_tmp[:, 1, :], scalar=0.25,
                                                    in1=ln_tmp[:, 1, :], op0=ALU.mult, op1=ALU.mult))
                nc.vector.scalar_tensor_tensor(out=ln_var[:, :], in0=ln_tmp[:, 2, :], scalar=1.0 / D,
                                               in1=ln_var[:, :], op0=ALU.mult, op1=ALU.add).then_inc(ln_var_ready, 1)
                for g in range(CENTRED[q], GROUPS):
                    for b in group_blocks(g):
                        last = nc.vector.tensor_scalar(rows_h[:, b, :], rows_x[:, b, :], ln_neg_mean[:, b:b + 1], 0.0,
                                                       ALU.add, ALU.max)
                    if g == GROUPS - 1:
                        link(last)
                dve.wait_ge(ln_std_ready, q + 1)
                link(nc.vector.reciprocal(ln_rstd[:, :], ln_rstd[:, :]))
                for g in range(GROUPS + LAG):
                    if g < GROUPS:
                        b0, nb = g * GB, len(group_blocks(g))
                        if g < CENTRED[q]:
                            dve.wait_ge(centred, q * CENTRED[0] + g + 1)
                        nc.vector.tensor_tensor(rows_h[:, b0:b0 + nb, :], rows_h[:, b0:b0 + nb, :],
                                                ln_rstd[:, b0:b0 + nb].unsqueeze(2).broadcast_to((P, nb, D)),
                                                ALU.mult).then_inc(rows_ready, 1)
                    if q == 1 and g >= LAG:
                        c0, w = group_cols(g - LAG)
                        dve.wait_ge(cols_turned, LG + g - LAG + 1)
                        nc.vector.tensor_scalar(acc[:, c0:c0 + w], psG[:, (g - LAG) % 4, 0:w], one_eps[:, 0:1], None,
                                                ALU.mult).then_inc(cols_ready, 1)

            def window_add(window, first, width):
                cols = acc[:, bass.DynSlice(first, width)]
                return nc.vector.tensor_tensor(cols, cols, window, ALU.add)

            def cell_rows(layer, k, c, supers):
                s = dve.snap(first_counted(layer, supers, k) + c)
                for j in range(EPP):
                    dve.wait_ge(cells_used, dve.snap(s * EPP + (j + 1)))
                    nc.vector.tensor_scalar(
                        src_hot[:, j, :], iota0[:, :],
                        src_lo_all[:, bass.DynSlice(s, 1), j:j + 1].rearrange("p o j -> p (o j)"), None, ALU.is_equal)
                    nc.vector.tensor_scalar(
                        cells[:, j, :], iota_c[:, :],
                        cell_all[:, bass.DynSlice(s, 1), j:j + 1].rearrange("p o j -> p (o j)"), None,
                        ALU.is_equal).then_inc(cells_ready, 1)

            def windows(layer, k, g, slots, super0):
                before = turns_before(layer, left)
                turn_rounds = dve.snap((k + before) * rounds)
                if layer >= 2:
                    gin_rounds = dve.snap((k + (layer - 2) * left) * rounds)
                    counts_before = dve.snap((k + (layer - 2) * left) * UPT + 1)
                others = slots[0] - 1 if g else SLOTS - 1
                others_added = dve.snap(turn_rounds + rounds + 1) if g else dve.snap(turn_rounds + 1)
                with dve.Fori(0, rounds) as r:
                    v = dve.snap(turn_rounds + r + 1)
                    nxt = dve.snap(v + 1)
                    nc.vector.tensor_scalar(first_i[:, slots[0]:slots[-1] + 1],
                                            base_f[:, bass.DynSlice(super0 + slots[0], len(slots))],
                                            round_off[0:1, bass.DynSlice(r, 1)], float(NODES),
                                            ALU.add, ALU.min).then_inc(firsts_ready[g], 1)

                    def add_window(u):
                        first = dve.value_load(first_i[0:1, u:u + 1], min_val=0, max_val=NODES)
                        dve.wait_ge(reduced[u], nxt)
                        if u > slots[0]:
                            dve.wait_ge(added[u - 1], nxt)
                        else:
                            dve.wait_ge(added[slots[-1]], v)
                            if len(slots) < SLOTS:
                                dve.wait_ge(added[others], others_added)
                            if layer >= 2 and u == 0:
                                dve.wait_ge(counts_added, counts_before)
                        window_add(psG[:, u, 0:WIN], first, WIN).then_inc(added[u], 1)

                    for u in slots:
                        if u == slots[0]:
                            dve.wait_ge(firsts_ready[g], dve.snap(gin_rounds + r + 1) if g else v)
                        dve.wait_ge(reduced[u], v)
                        loc = loc_all[:, bass.DynSlice(super0 + u, 1), :].rearrange("p o j -> p (o j)")
                        nc.vector.scalar_tensor_tensor(
                            out=hot[:, u, :, :], in0=loc.unsqueeze(2).broadcast_to((P, EPP, WIN)),
                            scalar=round_off[:, bass.DynSlice(r, 1)],
                            in1=iota0[:, :].unsqueeze(1).broadcast_to((P, EPP, WIN)),
                            op0=ALU.subtract, op1=ALU.is_equal).then_inc(hot_ready[u], 1)
                        if u > slots[0]:
                            add_window(u - 1)
                    add_window(slots[-1])

            def turns(layer, start, end, supers):
                before = turns_before(layer, left)
                with dve.Fori(start, end) as k:
                    n = dve.snap(k + before + 1)
                    super0 = dve.snap(k * SLOTS + (0 if layer < 2 else skipped * SLOTS)).with_bounds(min_val=0, max_val=SUPERS - SLOTS)
                    if layer < 2:
                        cell_rows(layer, k, 0, supers)
                        n16 = dve.snap(n * 16)
                        for u in range(SLOTS):
                            for j in range(EPP):
                                dve.wait_ge(gathered[u][j], n16)
                            dve.wait_ge(ea_loaded[u], n16)
                            nc.vector.tensor_tensor(ea[:, u, :, :], ea[:, u, :, :], xg[:, u, :, :],
                                                    ALU.add).then_inc(summed[u], 1)
                    for g, slots in enumerate(WINDOW_SLOTS[layer]):
                        windows(layer, k, g, slots, super0)
                        if layer >= 2 and g == 0:
                            group = dve.snap(k * use).with_bounds(min_val=0, max_val=TURNS - SKIP - 1)
                            firsts = [dve.value_load(unit_i[0:1, bass.DynSlice(group * UPT + w, 1)],
                                                     min_val=0, max_val=NODES) for w in range(UPT)]
                    if layer < 2 and supers == 2:
                        cell_rows(layer, k, 1, supers)
                    if layer >= 2:
                        m = dve.snap(k + (layer - 2) * left + 2)
                        for w, first in enumerate(firsts):
                            if w == 0:
                                dve.wait_ge(products_out, m)
                                dve.wait_ge(added[SLOTS - 1], dve.snap((k + before + 1) * rounds + 1))
                            else:
                                dve.wait_ge(counts_added, dve.snap((k + (layer - 2) * left) * UPT + (w + 1)))
                            window_add(product[:, w, :], first, CW).then_inc(counts_added, 1)

            def edges(layer):
                for start, end, supers in (BUILD_TURNS[layer] if layer < 2 else [(0, left, 0)]):
                    turns(layer, start, end, supers)

            def split_features(layer):
                for c in range(NSPLIT + 1):
                    if c < NSPLIT:
                        a, b = SPLIT[c]
                        dve.wait_ge(hi_ready, (layer - 2) * NSPLIT + c + 1)
                        nc.vector.scalar_tensor_tensor(out=hid_rows[:, a:b, :], in0=rows_h[:, a:b, :],
                                                       scalar=use_counts[:, 0:1], in1=xp[:, a:b, 0, :],
                                                       op0=ALU.mult, op1=ALU.subtract).then_inc(rest_ready, 1)
                    if c > 0:
                        a, b = SPLIT[c - 1]
                        dve.wait_ge(mid_ready, (layer - 2) * NSPLIT + c)
                        nc.vector.tensor_tensor(xp[:, a:b, 2, :], hid_rows[:, a:b, :], xp[:, a:b, 1, :],
                                                ALU.subtract).then_inc(parts_ready, 1)

            def mlp(layer):
                if layer < 2:
                    for g in range(GROUPS):
                        c0, _ = group_cols(g)
                        dve.wait_ge(hid_ready, layer * LG + g + 1)
                        last = nc.vector.bn_stats(bn_stats[:, g, :], hid[:, c0:c0 + real_cols(g)])
                    last.then_inc(bn_step, 1)
                    dve.wait_ge(bn_step, 4 * layer + 1)
                    nc.vector.bn_aggr(bn_mv[:, :], bn_stats[:, :, :].rearrange("p g k -> p (g k)")).then_inc(bn_var_ready, 1)
                    dve.wait_ge(bn_std_ready, layer + 1)
                    nc.vector.reciprocal(bn_tmp[:, :], bn_std[:, :]).then_inc(bn_step, 1)
                    dve.wait_ge(bn_step, 4 * layer + 2)
                    nc.vector.tensor_tensor(bn_scale[:, :], bn_tmp[:, :], bn_gamma[:, layer:layer + 1], ALU.mult).then_inc(bn_step, 1)
                    dve.wait_ge(bn_step, 4 * layer + 3)
                    nc.vector.tensor_tensor(bn_tmp[:, :], bn_mv[:, 0:1], bn_scale[:, :], ALU.mult).then_inc(bn_step, 1)
                    dve.wait_ge(bn_step, 4 * layer + 4)
                    nc.vector.tensor_tensor(bn_shift[:, :], bn_beta[:, layer:layer + 1], bn_tmp[:, :], ALU.subtract).then_inc(bn_ready, 1)
                if layer == 1:
                    for g in range(GROUPS + 1):
                        if g < GROUPS:
                            b0, nb = g * GB, len(group_blocks(g))
                            dve.wait_ge(rows_turned, layer * LG + g + 1)
                            nc.vector.tensor_tensor(rows_x[:, b0:b0 + nb, :], rows_x[:, b0:b0 + nb, :],
                                                    psG[:, g % 4, 0:nb * P].rearrange("p (b d) -> p b d", d=D), ALU.add
                                                    ).then_inc(resid_ready, 1)
                        if g > 0:
                            dve.wait_ge(resid_ready, g)
                            last = stats_of(g - 1)
                    link(last)
                elif layer == 3:
                    dve.wait_ge(table_written, 16 * LG * LAYERS)
                    dve.wait_ge(bias_added, 1)
                    for g in range(GROUPS):
                        b0, nb = g * GB, len(group_blocks(g))
                        dve.wait_ge(second_done, layer * LG + g + 1)
                        nc.vector.tensor_tensor(rows_h[:, b0:b0 + nb, :], rows_x[:, b0:b0 + nb, :],
                                                psA[:, g % 4, 0:nb * P].rearrange("p (b d) -> p b d", d=D), ALU.add
                                                ).then_inc(rows_ready, 1)
                else:
                    if layer == 2:
                        nc.vector.tensor_tensor(rows_x[:, :, :], rows_x[:, :, :],
                                                bias_last[:, :].unsqueeze(1).broadcast_to((P, BLOCKS, D)),
                                                ALU.add).then_inc(bias_added, 1)
                    behind = LAG + 1
                    for g in range(GROUPS + (behind if layer == 2 else 0)):
                        if g < GROUPS:
                            c0, w = group_cols(g)
                            dve.wait_ge(second_done, layer * LG + g + 1)
                            nc.vector.tensor_scalar(acc[:, c0:c0 + w], psA[:, g % 4, 0:w],
                                                    bias_second[:, layer:layer + 1], 0.0,
                                                    ALU.add, ALU.max).then_inc(next_ready, 1)
                        if layer == 2 and g >= behind:
                            c0, w = group_cols(g - behind)
                            dve.wait_ge(rows_turned, layer * LG + g - behind + 1)
                            nc.vector.tensor_scalar(acc[:, c0:c0 + w], acc[:, c0:c0 + w], one_eps[:, 1:2], None,
                                                    ALU.mult).then_inc(acc_scaled, 1)

            dve.wait_ge(pad_cleared, 1)
            for g in range(GROUPS):
                dve.wait_ge(x_loaded[g], 16)
                last = stats_of(g)
            link(last)
            norm_rows(0)
            dve.wait_ge(dst_loaded, 48)
            for h, rows in halves:
                f = flt[0:rows, 2 + h, :]
                st = win_stat[0:rows, h, :]
                link(nc.vector.tensor_copy(f, raw[0:rows, 2 + h, :]))
                link(nc.vector.tensor_reduce(st[:, 0:1], f, AX_X, ALU.min))
                link(nc.vector.tensor_reduce(st[:, 1:2], f, AX_X, ALU.max))
                nc.vector.tensor_tensor(st[:, 2:3], st[:, 1:2], st[:, 0:1], ALU.subtract).then_inc(stat_ready, 1)
                nc.vector.tensor_scalar(f, f, st[:, 0:1], None, ALU.subtract).then_inc(loc_float, 1)
            for h, rows in halves:
                dve.wait_ge(loc_turned, h + 1)
                nc.vector.tensor_copy(loc_all[:, h * FIRST:h * FIRST + rows, :].rearrange("p s j -> p j s"),
                                      psG[:, 2 + h, :].rearrange("p (j s) -> p j s", j=EPP)[:, :, 0:rows]
                                      ).then_inc(loc_ready, 1)
            dve.wait_ge(loc_ready, 2)
            link(nc.vector.memset(loc_all[0:OVERLAP // EPP, SUPERS - 1, :], -1.0))
            dve.wait_ge(base_turned, 1)
            link(nc.vector.tensor_copy(base_f[:, :], psA[0:1, 0, 0:SUPERS]))
            link(nc.vector.tensor_reduce(plan_f[:, 0:1], psA[0:1, 1, 0:SUPERS], AX_X, ALU.max))
            link(nc.vector.tensor_scalar(plan_f[:, 1:2], plan_f[:, 0:1], float(WIN), None, ALU.add))
            link(nc.vector.tensor_copy(rounds_wide[:, :], plan_f[:, 1:2]))
            nc.vector.tensor_scalar(plan_i[:, 0:1], rounds_wide[:, :], WIN.bit_length() - 1, None,
                                    ALU.arith_shift_right).then_inc(plan_ready, 1)
            link(nc.vector.tensor_tensor(last_f[:, :], base_f[:, 0:COUNTED], psA[0:1, 1, 0:COUNTED], ALU.add))
            pair = lambda t, k: t[:, 0:2 * PAIRS].rearrange("o (u k) -> o u k", k=2)[:, :, k]
            nc.vector.memset(unit_f[:, :, :], 0.0).then_inc(unit_step, 1)
            dve.wait_ge(unit_step, 1)
            nc.vector.tensor_tensor(unit_f[:, 0, 0:PAIRS], pair(base_f, 0), pair(base_f, 1), ALU.min).then_inc(unit_step, 1)
            nc.vector.tensor_copy(unit_f[:, 0, PAIRS:UNITS], base_f[:, 2 * PAIRS:COUNTED]).then_inc(unit_step, 1)
            nc.vector.tensor_tensor(unit_f[:, 1, 0:PAIRS], pair(last_f, 0), pair(last_f, 1), ALU.max).then_inc(unit_step, 1)
            nc.vector.tensor_copy(unit_f[:, 1, PAIRS:UNITS], last_f[:, 2 * PAIRS:COUNTED]).then_inc(unit_step, 1)
            dve.wait_ge(unit_step, 5)
            for k in range(2):
                nc.vector.tensor_tensor(pair(shift_f, k), pair(base_f, k), unit_f[:, 0, 0:PAIRS],
                                        ALU.subtract).then_inc(shift_ready, 1)
            nc.vector.tensor_copy(unit_i[:, :], unit_f[:, 0, :]).then_inc(unit_step, 1)
            link(nc.vector.tensor_tensor(unit_f[:, 2, :], unit_f[:, 1, :], unit_f[:, 0, :], ALU.subtract))
            link(nc.vector.tensor_reduce(plan_f[:, 2:3], unit_f[:, 2, :], AX_X, ALU.max))
            nc.vector.tensor_scalar(plan_f[:, 3:4], plan_f[:, 2:3], float(CW), None, ALU.is_lt).then_inc(flag_ready, 1)
            dve.wait_ge(flag_ready, 1)
            nc.vector.tensor_copy(plan_i[:, 3:4], plan_f[:, 3:4])
            nc.vector.tensor_scalar(plan_i[:, 1:2], plan_f[:, 3:4], float(SKIP), None, ALU.mult).then_inc(plan_ready, 1)
            nc.vector.tensor_scalar(plan_i[:, 2:3], plan_f[:, 3:4], -float(SKIP), float(TURNS), ALU.mult,
                                    ALU.add).then_inc(plan_ready, 1)
            dve.wait_ge(flag_turned, 2)
            nc.vector.tensor_copy(use_counts[:, :], psA[:, 2, 0:1]).then_inc(flag_ready, 1)
            dve.wait_ge(src_ready, 2)
            link(nc.vector.tensor_scalar(src_hi, src_all[:, 0:COUNTED, :], P.bit_length() - 1, None, ALU.arith_shift_right))
            link(nc.vector.tensor_scalar(src_lo, src_all[:, 0:COUNTED, :], P - 1, None, ALU.bitwise_and))
            link(nc.vector.scalar_tensor_tensor(out=cell_all[:, 0:COUNTED, :], in0=src_hi, scalar=float(CW),
                                                in1=loc_all[:, 0:COUNTED, :], op0=ALU.mult, op1=ALU.add))
            paired = cell_all[:, 0:2 * PAIRS, :]
            link(nc.vector.tensor_tensor(paired, paired,
                                         psA[:, 3, 0:2 * PAIRS].unsqueeze(2).broadcast_to((P, 2 * PAIRS, EPP)), ALU.add))
            link(nc.vector.tensor_copy(src_lo_all[:, :, :], src_lo))
            dve.wait_ge(params_loaded, PARAMS)
            for k in range(2):
                nc.vector.tensor_scalar(one_eps[:, k:k + 1], eps_col[:, k:k + 1], 1.0, None, ALU.add).then_inc(weights_ready, 1)
            rounds, skipped, left, use = load_plan(dve)
            dve.wait_ge(more_consts, 3)
            for layer in range(LAYERS):
                if layer in (0, 2):
                    dve.wait_ge(cols_ready, (layer // 2 + 1) * LG)
                    dve.wait_ge(consts_made, 5)
                elif layer == 1:
                    dve.wait_ge(next_ready, 1 * LG)
                else:
                    dve.wait_ge(acc_scaled, LG)
                if layer >= 2:
                    split_features(layer)
                edges(layer)
                mlp(layer)
                if layer == 1:
                    norm_rows(1)

        @block.tensor
        def _(pe):
            for u in range(SLOTS):
                pe.sem_inc(reduced[u], 1)
            pe.sem_inc(counted, 1)
            pe.sem_inc(cells_used, EPP)
            for h in range(2):
                pe.sem_inc(counts_used[h], 1)
            pe.wait_ge(consts_made, 5)

            def turn_indices(tables, ready, bank0, done):
                for h, rows in ((0, FIRST), (1, SECOND)):
                    pe.wait_ge(ready, h + 1)
                    for j in range(EPP):
                        last = nc.tensor.transpose(psG[:, bank0 + h, j * P:j * P + rows],
                                                   flt[0:rows, tables + h, j::EPP], ident[0:rows, 0:rows])
                    last.then_inc(done, 1)

            turn_indices(0, src_float, 0, src_turned)
            pe.wait_ge(src_ready, 2)

            def turn_rows(q):
                for g in range(GROUPS):
                    pe.wait_ge(rows_ready, (0, 2)[q] * LG + g + 1)
                    if g >= 4:
                        pe.wait_ge(cols_ready, q * LG + g - 3)
                    for k, b in enumerate(group_blocks(g)):
                        last = nc.tensor.transpose(psG[:, g % 4, k * P:(k + 1) * P], rows_h[:, b, :], ident[:, :])
                    last.then_inc(cols_turned, 1)

            def build_counts(layer, k, c, supers):
                s = first_counted(layer, supers, k) + c
                for j in range(EPP):
                    pe.wait_ge(cells_ready, pe.snap(s * EPP + (j + 1)))
                    for bank in range(CBANKS):
                        c0 = bank * 512
                        w = min(512, CB - c0)
                        last = nc.tensor.matmul(psA[:, bank, 0:w], src_hot[:, j, :], cells[:, j, c0:c0 + w],
                                                start=(c == 0 and j == 0), stop=(c == supers - 1 and j == EPP - 1))
                    last.then_inc(cells_used, 1)
                if c == supers - 1:
                    pe.wait_ge(cells_used, pe.snap(s * EPP + 2 * EPP))
                    pe.sem_inc(counted, 1)

            def multiply_counts(layer, k, h):
                out_cols = psA[:, 0, 0:UPT * CW].rearrange("p (s c) -> p s c", s=UPT)
                if h == 0:
                    pe.wait_ge(products_out, pe.snap(k + (layer - 2) * left + 1))
                pe.wait_ge(parts_ready, (layer - 2) * NSPLIT + (2, NSPLIT)[h])
                pe.wait_ge(counts_loaded[h], pe.snap((k + (layer - 2) * left + 1) * 16))
                for b in (range(0, HALF_B), range(HALF_B, BLOCKS))[h]:
                    for part in range(PARTS):
                        last = nc.tensor.matmul(out_cols, xp[:, b, part, :], counts[:, :, b * CW:(b + 1) * CW],
                                                start=(b == 0 and part == 0), stop=(b == BLOCKS - 1 and part == PARTS - 1))
                last.then_inc(counts_used[h], 1)

            def windows(layer, k, slots):
                before = turns_before(layer, left)
                n = pe.snap(k + before + 1)
                n16 = pe.snap(n * 16)
                with pe.Fori(0, rounds) as r:
                    v = pe.snap((k + before) * rounds + r + 1)
                    for u in slots:
                        pe.wait_ge(added[u], v)
                        pe.wait_ge(hot_ready[u], v)
                        if layer < 2:
                            pe.wait_ge(msg_ready[u], n)
                        for j in range(EPP):
                            if layer >= 2:
                                pe.wait_ge(gathered[u][j], n16)
                            msg = ea if layer < 2 else xg
                            last = nc.tensor.matmul(psG[:, u, 0:WIN], msg[:, u, j, :], hot[:, u, j, :],
                                                    start=(j == 0), stop=(j == EPP - 1))
                        last.then_inc(reduced[u], 1)

            def edges(layer):
                for start, end, supers in (BUILD_TURNS[layer] if layer < 2 else [(0, left, 0)]):
                    turns(layer, start, end, supers)

            def turns(layer, start, end, supers):
                with pe.Fori(start, end) as k:
                    if layer < 2:
                        pe.wait_ge(count_evicted, pe.snap(k + (layer * TURNS + 1)))
                        build_counts(layer, k, 0, supers)
                        windows(layer, k, WINDOW_SLOTS[layer][0])
                        if supers == 2:
                            build_counts(layer, k, 1, supers)
                    else:
                        for h in range(2):
                            multiply_counts(layer, k, h)
                            windows(layer, k, WINDOW_SLOTS[layer][h])

            def mlp(layer):
                for u in range(SLOTS):
                    pe.wait_ge(added[u], pe.snap(rounds * turns_before(layer + 1, left) + 1))
                if layer < 2:
                    pe.wait_ge(count_evicted, (layer + 1) * TURNS + 1)
                else:
                    pe.wait_ge(counts_added, pe.snap(left * (UPT * (layer - 1)) + 1))
                if layer < 2:
                    for g in range(GROUPS):
                        first_product(layer, g, g % 4, 4)
                    for g in range(GROUPS + LAG):
                        if g < GROUPS:
                            second_product(layer, g)
                        if g >= LAG:
                            to_rows(layer, g - LAG, (g - LAG) % 4, 4)
                elif layer == 2:
                    for g in range(GROUPS + 2 * LAG):
                        if g < GROUPS:
                            first_product(layer, g, g % 2, 2)
                        if LAG <= g < GROUPS + LAG:
                            second_product(layer, g - LAG)
                        if g >= 2 * LAG:
                            to_rows(layer, g - 2 * LAG, 2 + g % 2, 2)
                else:
                    for g in range(GROUPS + LAG):
                        if g < GROUPS:
                            first_product(layer, g, g % 4, 4)
                        if g >= LAG:
                            last_product(layer, g - LAG)

            def first_product(layer, g, bank, banks):
                c0, w = group_cols(g)
                if g >= banks:
                    pe.wait_ge(hid_ready, layer * LG + g - banks + 1)
                nc.tensor.matmul(psG[:, bank, 0:w], w_first[:, layer, :], acc[:, c0:c0 + w],
                                 start=True, stop=True).then_inc(first_done, 1)

            def second_product(layer, g):
                c0, w = group_cols(g)
                pe.wait_ge(act_ready if layer < 2 else hid_ready, layer * LG + g + 1)
                if g >= 4:
                    pe.wait_ge(next_ready, layer * LG + g - 3)
                nc.tensor.matmul(psA[:, g % 4, 0:w], w_second[:, layer, :], hid[:, c0:c0 + w],
                                 start=True, stop=True).then_inc(second_done, 1)

            def last_product(layer, g):
                pe.wait_ge(hid_ready, layer * LG + g + 1)
                if g >= 4:
                    pe.wait_ge(rows_ready, LAYERS * LG + g - 3)
                for k, b in enumerate(group_blocks(g)):
                    last = nc.tensor.matmul(psA[:, g % 4, k * P:(k + 1) * P], hid[:, b * P:(b + 1) * P],
                                            w_second[:, layer, :], start=True, stop=True)
                last.then_inc(second_done, 1)

            def to_rows(layer, g, bank, banks):
                pe.wait_ge(next_ready, layer * LG + g + 1)
                if g >= banks:
                    pe.wait_ge(resid_ready if layer == 1 else rows_ready, {0: 1, 1: 0, 2: 3}[layer] * LG + g - banks + 1)
                else:
                    pe.wait_ge(hid_ready, (layer + 1) * LG if layer < 2 else layer * LG + g + 1)
                for k, b in enumerate(group_blocks(g)):
                    last = nc.tensor.transpose(psG[:, bank, k * P:(k + 1) * P], acc[:, b * P:(b + 1) * P], ident[:, :])
                last.then_inc(rows_turned, 1)

            turn_rows(0)
            pe.wait_ge(params_loaded, PARAMS)
            pe.wait_ge(cols_ready, LG)
            for k in range(4):
                last = nc.tensor.transpose(psG[:, 1, k * P:(k + 1) * P], w_rows[:, k, :], ident[:, :])
            last.then_inc(weights_turned, 1)
            turn_indices(2, loc_float, 2, loc_turned)
            pe.wait_ge(stat_ready, 2)
            for h, rows in ((0, FIRST), (1, SECOND)):
                for k, col in ((0, 0), (1, 2)):
                    last = nc.tensor.matmul(psA[0:1, k, h * FIRST:h * FIRST + rows], win_stat[0:rows, h, col:col + 1],
                                            ident[0:rows, 0:rows], start=(h == 0), stop=True, skip_group_check=True)
            last.then_inc(base_turned, 1)
            pe.wait_ge(flag_ready, 1)
            pe.wait_ge(more_consts, 3)
            pe.wait_ge(shift_ready, 2)
            nc.tensor.matmul(psA[:, 3, 0:2 * PAIRS], ones_row[0:1, :], shift_f[0:1, :], start=True, stop=True).then_inc(flag_turned, 1)
            nc.tensor.matmul(psA[:, 2, 0:1], ones_row[0:1, :], plan_f[0:1, 3:4], start=True, stop=True).then_inc(flag_turned, 1)
            pe.wait_ge(loc_ready, 2)
            pe.wait_ge(weights_ready, 6)
            pe.wait_ge(flag_ready, 2)
            rounds, skipped, left, use = load_plan(pe)
            for layer in range(LAYERS):
                edges(layer)
                mlp(layer)
                if layer == 1:
                    turn_rows(1)


_INS = ['x', 'src', 'dst', 'edge_attr_128', 'L0_gnn_W1', 'L0_gnn_b1', 'L0_gnn_gamma', 'L0_gnn_beta', 'L0_gnn_W2',
        'L0_gnn_b2', 'L1_gnn_w1a', 'L1_gnn_b1a', 'L1_gnn_w1b', 'L1_gnn_b1b', 'L1_gnn_eps1', 'L1_gnn_w2a',
        'L1_gnn_b2a', 'L1_gnn_w2b', 'L1_gnn_b2b', 'L1_gnn_eps2']


def kernel(**inputs):
    import numpy as _np
    import concourse.bacc as _bacc
    from concourse import mybir as _mybir
    from concourse.bass_utils import run_bass_kernel_spmd as _run

    nc = _bacc.Bacc("TRN2", target_bir_lowering=False, num_devices=1)
    arrays, args = {}, []
    for name in _INS:
        a = _np.ascontiguousarray(_np.atleast_1d(_np.asarray(inputs[name])))
        arrays[f"in_{name}_dram"] = a
        args.append(nc.dram_tensor(f"in_{name}_dram", a.shape, _mybir.dt.from_np(a.dtype), kind="ExternalInput").ap())
    out = nc.dram_tensor("out_dram", (NODES, D), F32, kind="ExternalOutput").ap()
    gnn_kernel(nc, *args, out)
    r = _run(nc, [arrays], core_ids=[0])
    return r.results[0]["out_dram"]
```
